# Optimizing a Trainium2 kernel written in Bass

```python
import numpy as np
import jax
import jax.numpy as jnp

def _softmax(x, axis=-1):
    return jax.nn.softmax(x, axis=axis)

def _gelu(x):
    return jax.nn.gelu(x, approximate=True)

def _silu(x):
    return jax.nn.silu(x)

def _sigmoid(x):
    return jax.nn.sigmoid(x)

def _layernorm(x, axis=-1, eps=1e-05):
    m = jnp.mean(x, axis=axis, keepdims=True)
    v = jnp.var(x, axis=axis, keepdims=True)
    return (x - m) / jnp.sqrt(v + eps)

def _scatter_add(tgt, idx, src, axis=0):
    return tgt.at[idx].add(src)

def _segment_sum(src, seg, n):
    return jax.ops.segment_sum(src, seg, n)
kernel_name = 'mk_xattn_ffn_d2_seqx_r8_82fae3'

def setup_inputs(seed: int=0):
    np.random.seed(seed)
    _w = jnp.asarray

    def _rec_inputs():
        import jax
        import jax.numpy as jnp
        _rk = jax.random.key(seed)
        x = -0.0003929 + 0.9999 * jax.random.normal(jax.random.fold_in(_rk, 1), (64, 128, 128), jnp.float32)
        _lenS = 128 - jax.random.randint(jax.random.fold_in(_rk, 7), (64,), 0, max(1, 128 // 4) + 1, jnp.int32)
        _lenS2 = 120 - jax.random.randint(jax.random.fold_in(_rk, 8), (64,), 0, max(1, 120 // 4) + 1, jnp.int32)
        _ctx_1024P = jax.random.normal(jax.random.fold_in(_rk, 11), (64, 16, 128), jnp.float32)
        _ctx_1024c = jax.random.dirichlet(jax.random.fold_in(_rk, 511), 0.3 * jnp.ones((16,), jnp.float32), (64, 120))
        _ctx_1024t = jnp.einsum('bsk,bkd->bsd', _ctx_1024c, _ctx_1024P)
        _ctx_1024t = _ctx_1024t * jax.lax.rsqrt(jnp.mean(jnp.square(_ctx_1024t)) + 1e-12) * 0.953939
        ctx_1024 = 2.81802e-05 + 1.00001 * (_ctx_1024t + 0.3 * jax.random.normal(jax.random.fold_in(_rk, 611), (64, 120, 128), jnp.float32))
        return (x, ctx_1024)
    x, ctx_1024 = _rec_inputs()

    def _L0_xattn_setup():
        import jax, jax.numpy as jnp
        import numpy as np
        QUERY_DIM = 128
        HIDDEN_DIM = 128
        key = jax.random.key(seed)
        k1, k2, k3, k4 = jax.random.split(key, 4)
        query = jax.random.normal(k1, (8, 256, QUERY_DIM), dtype=jnp.float32)
        info = jax.random.normal(k2, (8, 256, HIDDEN_DIM), dtype=jnp.float32)
        bound = 1.0 / np.sqrt(QUERY_DIM)
        W = jax.random.uniform(k3, (HIDDEN_DIM, QUERY_DIM), jnp.float32, -bound, bound)
        b = jax.random.uniform(k4, (HIDDEN_DIM,), jnp.float32, -bound, bound)
        return {'query': query, 'info': info, 'W': W, 'b': b}
    _L0_xattn_all = _L0_xattn_setup()
    _L0_xattn_in = {k: v for k, v in _L0_xattn_all.items() if k in ('W', 'b')}
    del _L0_xattn_all

    def _L0_ffn_setup():
        import jax, jax.numpy as jnp
        import numpy as np
        H = 128
        I = 256
        E = 8
        B, S = (2, 128)

        def _swiglu(x, wg, wu, wd):
            return jax.nn.silu(x @ wg) * (x @ wu) @ wd
        key = jax.random.key(seed)
        ks = jax.random.split(key, 8)
        sc_h = 1.0 / np.sqrt(H)
        sc_i = 1.0 / np.sqrt(I)
        return {'hidden_states': jax.random.normal(ks[0], (B, S, H), jnp.float32), 'gate_w': jax.random.normal(ks[1], (H, E), jnp.float32) * sc_h, 'sh_gate': jax.random.normal(ks[2], (H, I), jnp.float32) * sc_h, 'sh_up': jax.random.normal(ks[3], (H, I), jnp.float32) * sc_h, 'sh_down': jax.random.normal(ks[4], (I, H), jnp.float32) * sc_i, 'rt_gate': jax.random.normal(ks[5], (E, H, I), jnp.float32) * sc_h, 'rt_up': jax.random.normal(ks[6], (E, H, I), jnp.float32) * sc_h, 'rt_down': jax.random.normal(ks[7], (E, I, H), jnp.float32) * sc_i}
    _L0_ffn_all = _L0_ffn_setup()
    _L0_ffn_in = {k: v for k, v in _L0_ffn_all.items() if k in ('gate_w', 'sh_gate', 'sh_up', 'sh_down', 'rt_gate', 'rt_up', 'rt_down')}
    del _L0_ffn_all

    def _L1_xattn_setup():
        import jax, jax.numpy as jnp
        import numpy as np
        B, S, D_IN, D_MODEL = (4, 256, 128, 128)
        key = jax.random.key(seed)
        ks = jax.random.split(key, 9)
        return {'q': jax.random.normal(ks[0], (B, S, D_IN), jnp.float32), 'k': jax.random.normal(ks[1], (B, S, D_IN), jnp.float32), 'v': jax.random.normal(ks[2], (B, S, D_IN), jnp.float32), 'Wq': jax.random.normal(ks[3], (D_IN, D_MODEL), jnp.float32) * 0.02, 'bq': jax.random.normal(ks[4], (D_MODEL,), jnp.float32) * 0.02, 'Wk': jax.random.normal(ks[5], (D_IN, D_MODEL), jnp.float32) * 0.02, 'bk': jax.random.normal(ks[6], (D_MODEL,), jnp.float32) * 0.02, 'Wv': jax.random.normal(ks[7], (D_IN, D_MODEL), jnp.float32) * 0.02, 'bv': jax.random.normal(ks[8], (D_MODEL,), jnp.float32) * 0.02}
    _L1_xattn_all = _L1_xattn_setup()
    _L1_xattn_in = {k: v for k, v in _L1_xattn_all.items() if k in ('Wq', 'bq', 'Wk', 'bk', 'Wv', 'bv')}
    del _L1_xattn_all

    def _L1_ffn_setup():
        import jax, jax.numpy as jnp
        import numpy as np
        DIM = 128
        DEPTH = 7
        PAR = 8
        N_NODES = 2 ** (DEPTH + 1) - 1
        WIDTH = PAR * N_NODES
        key = jax.random.key(seed)
        k1, k2, k3, k4 = jax.random.split(key, 4)
        init_k = float(np.sqrt(1.0 / DIM))
        init_k2 = float(np.sqrt(1.0 / ((DEPTH + 1) * PAR)))
        oldx = jax.random.normal(k1, (4, 256, DIM), dtype=jnp.float32)
        W_in = jax.random.uniform(k2, (WIDTH, DIM), jnp.float32, -init_k, init_k)
        b_in = jax.random.uniform(k3, (WIDTH,), jnp.float32, -init_k, init_k)
        W_out = jax.random.uniform(k4, (DIM, WIDTH), jnp.float32, -init_k2, init_k2)
        return {'oldx': oldx, 'W_in': W_in, 'b_in': b_in, 'W_out': W_out}
    _L1_ffn_all = _L1_ffn_setup()
    _L1_ffn_in = {k: v for k, v in _L1_ffn_all.items() if k in ('W_in', 'b_in', 'W_out')}
    del _L1_ffn_all
    return {'x': x, 'ctx_1024': ctx_1024, 'L0_xattn_W': _L0_xattn_in['W'], 'L0_xattn_b': _L0_xattn_in['b'], 'L0_ffn_gate_w': _L0_ffn_in['gate_w'], 'L0_ffn_sh_gate': _L0_ffn_in['sh_gate'], 'L0_ffn_sh_up': _L0_ffn_in['sh_up'], 'L0_ffn_sh_down': _L0_ffn_in['sh_down'], 'L0_ffn_rt_gate': _L0_ffn_in['rt_gate'], 'L0_ffn_rt_up': _L0_ffn_in['rt_up'], 'L0_ffn_rt_down': _L0_ffn_in['rt_down'], 'L1_xattn_Wq': _L1_xattn_in['Wq'], 'L1_xattn_bq': _L1_xattn_in['bq'], 'L1_xattn_Wk': _L1_xattn_in['Wk'], 'L1_xattn_bk': _L1_xattn_in['bk'], 'L1_xattn_Wv': _L1_xattn_in['Wv'], 'L1_xattn_bv': _L1_xattn_in['bv'], 'L1_ffn_W_in': _L1_ffn_in['W_in'], 'L1_ffn_b_in': _L1_ffn_in['b_in'], 'L1_ffn_W_out': _L1_ffn_in['W_out']}

def reference(x, ctx_1024, L0_xattn_W, L0_xattn_b, L0_ffn_gate_w, L0_ffn_sh_gate, L0_ffn_sh_up, L0_ffn_sh_down, L0_ffn_rt_gate, L0_ffn_rt_up, L0_ffn_rt_down, L1_xattn_Wq, L1_xattn_bq, L1_xattn_Wk, L1_xattn_bk, L1_xattn_Wv, L1_xattn_bv, L1_ffn_W_in, L1_ffn_b_in, L1_ffn_W_out):
    import jax
    import jax.numpy as jnp

    def _L0_xattn_ref(query, info, W, b):
        import jax, jax.numpy as jnp
        import numpy as np
        QUERY_DIM = 128
        HIDDEN_DIM = 128
        q = jnp.einsum('bsq,hq->bsh', query, W) + b
        scores = jax.nn.softmax(jnp.einsum('bsh,bmh->bsm', q, info), axis=-1)
        return jnp.einsum('bsm,bmh->bsh', scores, info)

    def _L0_ffn_ref(hidden_states, gate_w, sh_gate, sh_up, sh_down, rt_gate, rt_up, rt_down):
        import jax, jax.numpy as jnp
        import numpy as np
        H = 128
        I = 256
        E = 8
        B, S = (2, 128)

        def _swiglu(x, wg, wu, wd):
            return jax.nn.silu(x @ wg) * (x @ wu) @ wd
        b, s, h = hidden_states.shape
        x = hidden_states.reshape(-1, h)
        logits = x @ gate_w
        top_val = jnp.max(logits, axis=-1, keepdims=True)
        top_id = jnp.argmax(logits, axis=-1)
        score = jax.nn.sigmoid(top_val)
        xs = x * score
        g = jnp.einsum('th,ehi->eti', xs, rt_gate)
        u = jnp.einsum('th,ehi->eti', xs, rt_up)
        act = jax.nn.silu(g) * u
        y = jnp.einsum('eti,eih->eth', act, rt_down)
        onehot = jax.nn.one_hot(top_id, E, dtype=x.dtype)
        routed = jnp.einsum('eth,te->th', y, onehot)
        shared = _swiglu(x, sh_gate, sh_up, sh_down)
        return (shared + routed).reshape(b, s, h)

    def _L1_xattn_ref(q, k, v, Wq, bq, Wk, bk, Wv, bv):
        import jax, jax.numpy as jnp
        import numpy as np
        B, S, D_IN, D_MODEL = (4, 256, 128, 128)
        qp = jnp.einsum('bsd,de->bse', q, Wq) + bq
        kp = jnp.einsum('bsd,de->bse', k, Wk) + bk
        vp = jnp.einsum('bsd,de->bse', v, Wv) + bv
        scale = 1.0 / jnp.sqrt(jnp.asarray(kp.shape[-1], jnp.float32))
        logits = jnp.einsum('bqe,bke->bqk', qp, kp) * scale
        attn = jax.nn.softmax(logits, axis=-1)
        return jnp.einsum('bqk,bke->bqe', attn, vp)

    def _L1_ffn_ref(oldx, W_in, b_in, W_out):
        import jax, jax.numpy as jnp
        import numpy as np
        DIM = 128
        DEPTH = 7
        PAR = 8
        N_NODES = 2 ** (DEPTH + 1) - 1
        WIDTH = PAR * N_NODES
        x = oldx.reshape(-1, DIM)
        B = x.shape[0]
        logits = x @ W_in.T + b_in
        decisions = (logits > 0).astype(jnp.int32).reshape(B, PAR, N_NODES)
        acts = jax.nn.silu(logits).reshape(B, PAR, N_NODES)
        current = jnp.zeros((B, PAR), dtype=jnp.int32)
        dmap = jax.nn.one_hot(current, N_NODES, dtype=acts.dtype)
        for d in range(DEPTH):
            cur_platform = 2 ** d - 1
            next_platform = 2 ** (d + 1) - 1
            moves = jnp.take_along_axis(decisions, current[..., None], axis=2)[..., 0]
            current = (current - cur_platform) * 2 + moves + next_platform
            dmap = dmap + jax.nn.one_hot(current, N_NODES, dtype=acts.dtype)
        masked = acts * jax.lax.stop_gradient(dmap)
        out = masked.reshape(B, WIDTH) @ W_out.T
        return out.reshape(oldx.shape)
    x = x + _L0_xattn_ref(_layernorm(x, axis=-1), ctx_1024, L0_xattn_W, L0_xattn_b)
    x = x + _L0_ffn_ref(_layernorm(x, axis=-1), L0_ffn_gate_w, L0_ffn_sh_gate, L0_ffn_sh_up, L0_ffn_sh_down, L0_ffn_rt_gate, L0_ffn_rt_up, L0_ffn_rt_down)
    x = x + _L1_xattn_ref(_layernorm(x, axis=-1), ctx_1024, ctx_1024, L1_xattn_Wq, L1_xattn_bq, L1_xattn_Wk, L1_xattn_bk, L1_xattn_Wv, L1_xattn_bv)
    x = x + _L1_ffn_ref(_layernorm(x, axis=-1), L1_ffn_W_in, L1_ffn_b_in, L1_ffn_W_out)
    return x

_drawn_inputs = setup_inputs


def setup_inputs(seed=0):
    import zlib

    import numpy as np

    out = dict(_drawn_inputs(seed))
    spreads = {}
    factors = {'L1_xattn_Wq': 8.0,
     'L1_xattn_bq': 24.314,
     'L1_xattn_Wk': 8.0,
     'L1_xattn_bk': 64.0,
     'L1_xattn_bv': 2.679}
    for name, (base, spread) in spreads.items():
        noise = np.random.default_rng([zlib.crc32(name.encode()), seed]).standard_normal(out[name].shape)
        drawn = base * np.exp(spread * noise) if base else spread * noise
        out[name] = jnp.asarray(drawn.astype(out[name].dtype))
    for name, factor in factors.items():
        out[name] = (out[name] * factor).astype(out[name].dtype)
    return out
```

```python
from contextlib import ExitStack

import numpy as np

import concourse.bass as bass
from concourse import mybir

F32 = mybir.dt.float32
BF16 = mybir.dt.bfloat16
I32 = mybir.dt.int32
ALU = mybir.AluOpType
ACT = mybir.ActivationFunctionType
AX = mybir.AxisListType

P = 128
B = 64
KEYS = 120
G = 4
NG = B // G
W = G * P
KW = G * KEYS
E = 8
FI = 256
FC = FI // P
SLOT_TILES = B + E
NR = SLOT_TILES // G
TREES = 8
DEPTH = 7
BIG = float(2.0 ** 40)
EPS = 1e-5
SCALE = float(P) ** -0.5


def constants():
    ident = np.eye(P, dtype=np.float32)
    inner = np.zeros((P, P), np.float32)
    leaves = np.zeros((P, P), np.float32)
    for node in range(2 * P - 1):
        table, col = (inner, node) if node < P - 1 else (leaves, node - (P - 1))
        child = node
        while child > 0:
            parent = (child - 1) // 2
            if child == 2 * parent + 2:
                table[parent, col] += BIG
                table[P - 1, col] -= BIG
            else:
                table[parent, col] -= BIG
            child = parent
    before = np.triu(np.ones((P, P), np.float32), 1)
    rank = np.broadcast_to(np.arange(E, 0, -1, dtype=np.float32), (P, E))
    tile = np.broadcast_to(np.arange(SLOT_TILES, dtype=np.float32), (P, SLOT_TILES))
    keep = np.ones((P, E, B), np.float32)
    keep[:, :, 0] = 0.0
    return np.ascontiguousarray(np.concatenate([ident, inner, leaves, before, rank, tile, keep.reshape(P, E * B)], 1))


C_ID, C_IN, C_LV, C_BEF = 0, P, 2 * P, 3 * P
C_RANK = 4 * P
C_TILE = C_RANK + E
C_KEEP = C_TILE + SLOT_TILES
C_END = C_KEEP + E * B


def program(nc, x, ctx_kv, w0, b0, gate, sh_gate, sh_up, sh_down, rt_gate, rt_up, rt_down,
            wq, bq, wk, bk, wv, bv, w_in, b_in, w_out, const, out):
    x_sorted = nc.dram_tensor("x_sorted", (SLOT_TILES * P, P), F32, kind="Internal").ap()
    y_sorted = nc.dram_tensor("y_sorted", (SLOT_TILES * P, P), F32, kind="Internal").ap()
    with ExitStack() as ctx:
        def sb(name, shape, dt=F32):
            return ctx.enter_context(nc.sbuf_tensor(name, shape, dt))

        def sem(name):
            return ctx.enter_context(nc.semaphore(name))

        def sems(name, n):
            return [sem(f"{name}{i}") for i in range(n)]

        X = sb("X", [P, B * P])
        KT = sb("KT", [P, B * KEYS])
        V = sb("V", [KEYS, B * P])
        WA = sb("WA", [P, C_RANK])
        anc_in = sb("anc_in", [P, P], BF16)
        anc_lv = sb("anc_lv", [P, P], BF16)
        before = sb("before", [P, P], BF16)
        all_ones = sb("all_ones", [P, P], BF16)
        W0T = sb("W0T", [P, P])
        WQ = sb("WQ", [P, P])
        WK = sb("WK", [P, P])
        WV = sb("WV", [P, P])
        GATE = sb("GATE", [P, E])
        SGU = sb("SGU", [P, 2 * FI])
        SD = sb("SD", [P, FC * P])
        WIN = sb("WIN", [P, 2 * TREES * P])
        WOUT = sb("WOUT", [P, 2 * TREES * P])
        b_in_c = sb("b_in_c", [P, 2 * TREES])
        b0c = sb("b0c", [P, 1])
        bqc = sb("bqc", [P, 1])
        bkc = sb("bkc", [P, 1])
        bvr = sb("bvr", [KEYS, P])
        neg_half = sb("neg_half", [P, G])
        eps = sb("eps", [P, G])
        MEAN2 = sb("MEAN2", [P, B])
        RSTD2 = sb("RSTD2", [P, B])
        POS = sb("POS", [P, B], I32)
        EXPERT = sb("EXPERT", [P, SLOT_TILES], I32)
        LG = sb("LG", [P, B * E])
        RA = sb("RA", [P, 6656])
        RB = sb("RB", [P, B * P])
        RS = sb("RS", [P, 3072])
        st = sb("st", [P, 2, G, 6])
        mv = sb("mv", [P, 2, G, 2])
        ve = sb("ve", [P, 2, G])
        rs = sb("rs", [P, 2, G])
        nmax = sb("nmax", [P, G])
        nmax_s = sb("nmax_s", [P, G])
        ssum = sb("ssum", [P, G])
        srec = sb("srec", [P, G])
        idx = sb("idx", [P, 2, G], I32)
        PS = ctx.enter_context(nc.psum_tensor("PS", [P, 8 * 512], F32))

        def bank(i, n=512, parts=P):
            return PS[0:parts, 512 * i:512 * i + n]

        class Cut:
            def __init__(self, region):
                self.region, self.at = region, 0

            def take(self, n, parts=P):
                a = self.region[0:parts, self.at:self.at + n]
                self.at += n
                assert self.at <= self.region.shape[1]
                return a

        IDENT = WA[:, C_ID:C_ID + P]
        cut = Cut(RA)
        ctx_rows = [cut.take(W, KEYS) for _ in range(2)]
        ctxT = [cut.take(KW) for _ in range(2)]
        xn = cut.take(W)
        xnT = cut.take(W)
        qT = cut.take(W)
        prob = cut.take(KW)
        probT = cut.take(W, KEYS)
        xn2 = cut.take(W)
        xn2T_s = cut.take(W)
        zeros = cut.take(P)
        c_rout = cut.take(C_END - C_RANK)
        XN2T = RB
        cut = Cut(RA)
        lead = cut.take(B * E)
        onehot = cut.take(B * E)
        slot = cut.take(B * E)
        counts = cut.take(B * E)
        upto = cut.take(B * E)
        top = cut.take(B)
        best = cut.take(B)
        posf = cut.take(B)
        score = cut.take(B)
        tiles_i = cut.take(E).bitcast(I32)
        tiles_f = cut.take(E)
        tile_end = cut.take(E)
        first_slot = cut.take(E)
        passed = cut.take(SLOT_TILES * E)
        expert_f = cut.take(SLOT_TILES)
        onehot_b = cut.take(B * E // 2).bitcast(BF16)
        assert cut.at <= 6656 - P - (C_END - C_RANK)
        cut = Cut(RA)
        WGU = cut.take(E * 2 * FI)
        WD = cut.take(E * FC * P)
        cut = Cut(RS)
        s_act = [cut.take(FC * W) for _ in range(2)]
        xs = [cut.take(W) for _ in range(2)]
        cut = Cut(RB)
        xs_in = [cut.take(W) for _ in range(2)]
        xsT = [cut.take(W) for _ in range(2)]
        sg = [cut.take(2 * FI) for _ in range(2)]
        ract = [cut.take(2 * FI) for _ in range(2)]
        actT = [cut.take(2 * FI) for _ in range(2)]
        yo = [cut.take(W) for _ in range(2)]
        cut = Cut(RB)
        sil = [cut.take(2 * W) for _ in range(2)]
        x4T = [cut.take(W) for _ in range(2)]
        ys = [cut.take(W) for _ in range(2)]
        xn3 = cut.take(W)
        xn3T = cut.take(W)
        q1T = cut.take(W)
        prob1 = cut.take(KW)
        prob1T = cut.take(W, KEYS)
        accT = cut.take(W)
        cut = Cut(RS)
        dec = [cut.take(W // 2).bitcast(BF16) for _ in range(2)]
        res = [cut.take(W) for _ in range(2)]

        consts_in, w_a, w_s, w_exp, w_tree = sem("consts_in"), sem("w_a"), sem("w_s"), sem("w_exp"), sem("w_tree")
        x_in, c_in = sems("x_in", 2), sems("c_in", 2)
        cast_done, zero_done, zeroed, half_done, ones_done = (
            sem("cast_done"), sem("zero_done"), sem("zeroed"), sem("half_done"), sem("ones_done"))
        a_ctxT_ps, a_ctxT = sem("a_ctxT_ps"), sem("a_ctxT")
        a_k_ps, a_k, a_v_ps, a_v = sem("a_k_ps"), sem("a_k"), sem("a_v_ps"), sem("a_v")
        a_st1, a_mv1, a_ve1, a_rs1, a_xn = sem("a_st1"), sem("a_mv1"), sem("a_ve1"), sem("a_rs1"), sem("a_xn")
        a_xnT_ps, a_xnT, a_qT_ps, a_qT = sem("a_xnT_ps"), sem("a_xnT"), sem("a_qT_ps"), sem("a_qT")
        a_s_ps, a_max, a_exp, a_pT_ps, a_pT = sem("a_s_ps"), sem("a_max"), sem("a_exp"), sem("a_pT_ps"), sem("a_pT")
        a_pv_ps, a_rec, a_x1 = sem("a_pv_ps"), sem("a_rec"), sem("a_x1")
        a_st2, a_mv2, a_ve2, a_rs2, a_xn2 = sem("a_st2"), sem("a_mv2"), sem("a_ve2"), sem("a_rs2"), sem("a_xn2")
        a_mean, a_copied = sem("a_mean"), sem("a_copied")
        a_x2T_ps, a_x2T, a_lg_ps, a_lg = sem("a_x2T_ps"), sem("a_x2T"), sem("a_lg_ps"), sem("a_lg")
        top_done = sem("top_done")
        dve_passed, pool_passed = sem("dve_passed"), sem("pool_passed")
        route, r_oh, r_cnt, scored, routed, pos_done = (
            sem("route"), sem("r_oh"), sem("r_cnt"), sem("scored"), sem("routed"), sem("pos_done"))
        s_gu_ps, s_sil, s_act_d, s_y_ps, s_add = (
            sem("s_gu_ps"), sem("s_sil"), sem("s_act_d"), sem("s_y_ps"), sem("s_add"))
        s_xs, s_idx, scattered = sem("s_xs"), sem("s_idx"), sem("scattered")
        r_in = sems("r_in", 2)
        r_xT_ps, r_xT, r_gu_ps, r_sg, r_act, r_aT_ps, r_aT, r_y_ps, r_y = (
            sem("r_xT_ps"), sem("r_xT"), sem("r_gu_ps"), sem("r_sg"), sem("r_act"), sem("r_aT_ps"), sem("r_aT"),
            sem("r_y_ps"), sem("r_y"))
        r_out = sems("r_out", 2)
        c_idx, y_in = sem("c_idx"), sems("y_in", 2)
        c_x2, c_st3, c_mv3, c_ve3, c_rs3, c_xn3 = (
            sem("c_x2"), sem("c_st3"), sem("c_mv3"), sem("c_ve3"), sem("c_rs3"), sem("c_xn3"))
        c_xnT_ps, c_xnT, c_qT_ps, c_qT = sem("c_xnT_ps"), sem("c_xnT"), sem("c_qT_ps"), sem("c_qT")
        c_s_ps, c_max, c_maxs, c_exp, c_pT_ps, c_pT, c_pv_ps, c_rec, c_x3 = (
            sem("c_s_ps"), sem("c_max"), sem("c_maxs"), sem("c_exp"), sem("c_pT_ps"), sem("c_pT"), sem("c_pv_ps"),
            sem("c_rec"), sem("c_x3"))
        c_st4, c_mv4, c_ve4, c_rs4, c_xn4 = sem("c_st4"), sem("c_mv4"), sem("c_ve4"), sem("c_rs4"), sem("c_xn4")
        c_x4T_ps, c_x4T = sem("c_x4T_ps"), sem("c_x4T")
        t_in, t_dec, t_mask, t_sil, t_out, t_acc, t_accT, t_res = (
            sem("t_in"), sem("t_dec"), sem("t_mask"), sem("t_sil"), sem("t_out"), sem("t_acc"), sem("t_accT"),
            sem("t_res"))
        stored = sems("stored", 2)

        block = ctx.enter_context(nc.Block())

        def cols(a, start, n):
            return a[:, start:start + n] if isinstance(start, int) else a[:, bass.ds(start, n)]

        def tile(a, j, n=P):
            return a[:, j * n:(j + 1) * n]

        def by_tile(a, n=P):
            return a.rearrange("p (t n) -> p t n", n=n)

        def first(g):
            return isinstance(g, int) and g == 0

        def last_g(g):
            return isinstance(g, int) and g == NG - 1

        def last_r(r):
            return isinstance(r, int) and r == NR - 1

        def phase_a(eng, body):
            body(0, None, None, 0)
            body(1, 0, None, 1)
            with eng.Fori(0, NG // 2 - 1) as i:
                body(2 * i + 2, 2 * i + 1, 2 * i, 0)
                body(2 * i + 3, 2 * i + 2, 2 * i + 1, 1)
            body(None, NG - 1, NG - 2, 0)
            body(None, None, NG - 1, 1)

        def phase_c(eng, body):
            body(0, 0)
            with eng.Fori(0, NG // 2 - 1) as i:
                body(2 * i + 1, 1)
                body(2 * i + 2, 0)
            body(NG - 1, 1)

        def half(g):
            return g // 2

        A_WEIGHTS = [(WA[:, :], const[:, 0:C_RANK]), (c_rout, const[:, C_RANK:C_END]),
                     (W0T[:, :], w0), (b0c[:, :], b0.rearrange("(p a) -> p a", a=1)), (WK[:, :], wk),
                     (bkc[:, :], bk.rearrange("(p a) -> p a", a=1)), (WV[:, :], wv),
                     (bvr[:, :], bv.partition_broadcast(KEYS)), (GATE[:, :], gate), (WQ[:, :], wq),
                     (bqc[:, :], bq.rearrange("(p a) -> p a", a=1)), (SGU[:, 0:FI], sh_gate), (SGU[:, FI:], sh_up),
                     (by_tile(SD[:, :]), sh_down.rearrange("(c i) h -> i c h", c=FC)),
                     (WIN[:, :], w_in), (by_tile(WOUT[:, :]), w_out.rearrange("(c i) h -> i c h", c=2 * TREES)),
                     (b_in_c[:, :], b_in)]

        @block.sync
        def _(sp):
            def load_group(g, u):
                sp.dma_start(by_tile(cols(X, g * W, W)),
                             x[bass.ds(g * G, G), :, :].rearrange("b s d -> s b d")).then_inc(x_in[u], 16)
                sp.dma_start(by_tile(ctx_rows[u]),
                             ctx_kv[bass.ds(g * G, G), :, :].rearrange("b s d -> s b d")).then_inc(c_in[u], 16)

            for u in range(2):
                sp.sem_inc(r_out[u], 16)
                sp.sem_inc(stored[u], 16)
            load_group(0, 0)
            load_group(1, 1)
            sp.wait_ge(zero_done, 1)
            for i in range(SLOT_TILES):
                sp.dma_start(x_sorted[i * P:(i + 1) * P, :], zeros).then_inc(zeroed, 16)
            with sp.Fori(0, NG // 2 - 1) as i:
                for u in range(2):
                    sp.wait_ge(a_pv_ps, 2 * i + u + 1)
                    load_group(2 * i + u + 2, u)
            sp.wait_ge(pos_done, 1)
            sp.wait_ge(a_copied, NG)
            sp.wait_ge(zeroed, 16 * SLOT_TILES)
            gu = WGU.rearrange("p (e n) -> p e n", e=E)
            sp.dma_start(gu[:, :, 0:FI], rt_gate.rearrange("e h i -> h e i")).then_inc(w_exp, 16)
            sp.dma_start(gu[:, :, FI:], rt_up.rearrange("e h i -> h e i")).then_inc(w_exp, 16)
            sp.dma_start(by_tile(WD), rt_down.rearrange("e (c i) h -> i (e c) h", c=FC)).then_inc(w_exp, 16)

            def r_load(r, u):
                sp.dma_start(by_tile(xs_in[u]),
                             x_sorted[bass.ds(r * W, W), :].rearrange("(t p) d -> p t d", p=P)).then_inc(r_in[u], 16)

            def r_store(r, u):
                sp.wait_ge(r_y, r + 1)
                sp.dma_start(y_sorted[bass.ds(r * W, W), :].rearrange("(t p) d -> p t d", p=P),
                             by_tile(yo[u])).then_inc(r_out[u], 16)

            sp.wait_ge(scattered, 16 * B)
            sp.wait_ge(s_gu_ps, 2 * NG)
            r_load(0, 0)
            r_load(1, 1)
            with sp.Fori(0, NR // 2 - 1) as i:
                for u in range(2):
                    sp.wait_ge(r_xT_ps, 2 * i + u + 1)
                    r_load(2 * i + u + 2, u)
                    r_store(2 * i + u, u)
            for r in (NR - 2, NR - 1):
                r_store(r, r % 2)

            def store(g, u):
                sp.wait_ge(t_res, g + 1)
                sp.dma_start(out[bass.ds(g * G, G), :, :].rearrange("b s d -> s b d"),
                             by_tile(res[u])).then_inc(stored[u], 16)

            with sp.Fori(0, NG // 2) as i:
                for u in range(2):
                    store(2 * i + u, u)
            for u in range(2):
                sp.wait_ge(stored[u], 16 * (NG // 2 + 1))

        @block.gpsimd
        def _(pool):
            pool.memset(neg_half[:, :], -0.5).then_inc(half_done, 1)
            pool.memset(zeros, 0.0).then_inc(zero_done, 1)
            pool.memset(all_ones[:, :], 1.0).then_inc(ones_done, 1)
            pool.memset(eps[:, :], EPS).then_inc(half_done, 1)
            pool.wait_ge(half_done, 2)

            def rstd(s, g, mv_done, ve_done, rs_done):
                pool.wait_ge(mv_done, g + 1)
                pool.tensor_tensor(ve[:, s, :], mv[:, s, :, 1], eps[:, :], ALU.add).then_inc(ve_done, 1)
                pool.wait_ge(ve_done, g + 1)
                pool.tensor_tensor(rs[:, s, :], ve[:, s, :], neg_half[:, :], ALU.pow).then_inc(rs_done, 1)

            def late(g):
                rstd(1, g, a_mv2, a_ve2, a_rs2)
                pool.wait_ge(a_rs2, g + 1)
                pool.tensor_copy(cols(RSTD2, g * G, G), rs[:, 1, :])
                pool.tensor_copy(cols(MEAN2, g * G, G), mv[:, 1, :, 0]).then_inc(a_mean, 1)

            def keep_rows(g):
                pool.wait_ge(a_x2T, g + 1)
                pool.tensor_copy(cols(XN2T, g * W, W), xn2T_s).then_inc(a_copied, 1)

            rstd(0, 0, a_mv1, a_ve1, a_rs1)
            rstd(0, 1, a_mv1, a_ve1, a_rs1)
            late(0)
            with pool.Fori(1, NG - 1) as g:
                rstd(0, g + 1, a_mv1, a_ve1, a_rs1)
                keep_rows(g - 1)
                late(g)
            keep_rows(NG - 2)
            late(NG - 1)
            keep_rows(NG - 1)

            pool.wait_ge(routed, 1)
            pool.wait_ge(zeroed, 16 * SLOT_TILES)
            def scatter(g, u):
                pool.tensor_copy(idx[:, u, :], cols(POS, g * G, G)).then_inc(s_idx, 1)
                pool.wait_ge(s_idx, g + 1)
                pool.wait_ge(s_xs, g + 1)
                pool.sem_inc(pool_passed, 1)
                for j in range(G):
                    pool.indirect_dma_start(x_sorted, bass.IndirectOffsetOnAxis(ap=idx[:, u, j:j + 1], axis=0),
                                            tile(xs[u], j), None).then_inc(scattered, 16)

            scatter(0, 0)
            pool.wait_ge(scattered, 16 * G)
            scatter(1, 1)
            with pool.Fori(1, NG // 2) as i:
                for u in range(2):
                    pool.wait_ge(scattered, 16 * G * (2 * i + u))
                    scatter(2 * i + u, u)

            for u in range(2):
                pool.wait_ge(r_out[u], 16 * (NR // 2 + 1))
            pool.wait_ge(scattered, 16 * B)

            def gather(h, u):
                pool.tensor_copy(idx[:, u, :], cols(POS, h * G, G)).then_inc(c_idx, 1)
                pool.wait_ge(c_idx, h + 1)
                pool.sem_inc(pool_passed, 1)
                for j in range(G):
                    pool.indirect_dma_start(tile(ys[u], j), None, y_sorted,
                                            bass.IndirectOffsetOnAxis(ap=idx[:, u, j:j + 1], axis=0)
                                            ).then_inc(y_in[u], 16)

            gather(0, 0)
            gather(1, 1)

            def c_rstd(h, u, more):
                rstd(0, h, c_mv3, c_ve3, c_rs3)
                if more:
                    pool.wait_ge(c_x2, h + 1)
                    gather(h + 2, u)
                rstd(1, h, c_mv4, c_ve4, c_rs4)

            with pool.Fori(0, NG // 2 - 1) as i:
                for u in range(2):
                    c_rstd(2 * i + u, u, True)
            for h in (NG - 2, NG - 1):
                c_rstd(h, h % 2, False)

        @block.scalar
        def _(act):
            for dst, src in A_WEIGHTS:
                act.dma_start(dst, src).then_inc(w_a, 16)

            def a_body(f, g, l, u):
                if f is not None:
                    act.wait_ge(a_ctxT_ps, f + 1)
                    act.activation(ctxT[u], bank(0, KW), ACT.Copy).then_inc(a_ctxT, 1)
                if g is not None:
                    act.wait_ge(a_max, g + 1)
                    if not first(g):
                        act.wait_ge(a_pT_ps, g)
                        act.wait_ge(a_x1, g)
                    for j in range(G):
                        i = act.activation(tile(prob, j, KEYS), tile(bank(1, KW), j, KEYS), ACT.Exp,
                                           bias=nmax[:, j:j + 1], accum_out=ssum[:, j:j + 1])
                    i.then_inc(a_exp, 1)
                if l is not None:
                    act.wait_ge(a_x2T_ps, l + 1)
                    if not first(l):
                        act.wait_ge(a_lg_ps, l)
                        act.wait_ge(a_copied, l)
                    act.activation(xn2T_s, bank(4), ACT.Copy).then_inc(a_x2T, 1)
                if f is not None:
                    act.wait_ge(a_k_ps, f + 1)
                    act.activation(cols(KT, f * KW, KW), bank(2, KW), ACT.Identity, bias=bkc[:, :]).then_inc(a_k, 1)
                    act.wait_ge(a_xnT_ps, f + 1)
                    act.activation(xnT, bank(5), ACT.Copy).then_inc(a_xnT, 1)
                    act.wait_ge(a_qT_ps, f + 1)
                    act.activation(qT, bank(7), ACT.Identity, bias=b0c[:, :]).then_inc(a_qT, 1)

            act.wait_ge(w_a, 16 * len(A_WEIGHTS))
            phase_a(act, a_body)

            act.wait_ge(top_done, 1)
            act.activation(score, top, ACT.Sigmoid).then_inc(scored, 1)

            def s_silu(g, u):
                for c in range(FC):
                    act.wait_ge(s_gu_ps, FC * g + c + 1)
                    if not (isinstance(g, int) and g < 2):
                        act.wait_ge(s_y_ps, g - 1)
                    act.activation(tile(s_act[u], c, W), bank(2 * c), ACT.Silu).then_inc(s_sil, 1)

            s_silu(0, 0)
            s_silu(1, 1)
            with act.Fori(1, NG // 2) as i:
                for u in range(2):
                    s_silu(2 * i + u, u)

            def r_evac_x(r, u):
                act.wait_ge(r_xT_ps, r + 1)
                act.activation(xsT[u], bank(0), ACT.Copy).then_inc(r_xT, 1)

            def r_silu(q, v):
                act.wait_ge(r_gu_ps, q + 1)
                pair = by_tile(PS[:, 512 * (1 + 2 * v):512 * (3 + 2 * v)], 512)
                act.activation(by_tile(sg[v], FI), pair[:, :, 0:FI], ACT.Silu).then_inc(r_sg, 1)

            def r_evac_y(r, u, stores):
                act.wait_ge(r_y_ps, 2 * r + 2)
                act.wait_ge(r_out[u], 16 * (stores + 1))
                act.activation(yo[u], bank(6 + u), ACT.Copy).then_inc(r_y, 1)

            def r_body(r, u, stores):
                if not last_r(r):
                    r_evac_x(r + 1, 1 - u)
                r_silu(2 * r, 0)
                if not first(r):
                    r_evac_y(r - 1, 1 - u, stores)
                r_silu(2 * r + 1, 1)

            r_evac_x(0, 0)
            r_body(0, 0, None)
            with act.Fori(0, NR // 2 - 1) as i:
                r_body(2 * i + 1, 1, i)
                r_body(2 * i + 2, 0, i)
            r_body(NR - 1, 1, NR // 2 - 1)
            r_evac_y(NR - 1, 1, NR // 2 - 1)

            def c_xnT_evac(h):
                act.wait_ge(c_xnT_ps, h + 1)
                act.activation(xn3T, bank(5), ACT.Copy).then_inc(c_xnT, 1)

            def c_qT_evac(h):
                act.wait_ge(c_qT_ps, h + 1)
                act.activation(q1T, bank(6), ACT.Identity, bias=bqc[:, :]).then_inc(c_qT, 1)

            def c_softmax(h):
                act.wait_ge(c_maxs, h + 1)
                for j in range(G):
                    i = act.activation(tile(prob1, j, KEYS), tile(bank(7, KW), j, KEYS), ACT.Exp, scale=SCALE,
                                       bias=nmax_s[:, j:j + 1], accum_out=ssum[:, j:j + 1])
                i.then_inc(c_exp, 1)

            def c_x4T_evac(h, u):
                act.wait_ge(c_x4T_ps, h + 1)
                act.activation(x4T[u], bank(7), ACT.Copy).then_inc(c_x4T, 1)

            def t_silu(g, p):
                q = TREES * g + p
                act.wait_ge(t_mask, q + 1)
                if not (isinstance(q, int) and q < 2):
                    act.wait_ge(t_out, q - 1)
                for c in range(2):
                    i = act.activation(tile(sil[p % 2], c, W), bank(2 * (p % 2) + c), ACT.Silu,
                                       bias=b_in_c[:, 2 * p + c:2 * p + c + 1])
                i.then_inc(t_sil, 1)

            def t_acc_evac(g):
                act.wait_ge(t_out, TREES * g + TREES)
                if not first(g):
                    act.wait_ge(t_acc, g)
                act.activation(accT, bank(4), ACT.Copy).then_inc(t_accT, 1)

            def c_body(g, u):
                for p in range(TREES):
                    t_silu(g, p)
                    if p == 0 and not first(g):
                        t_acc_evac(g - 1)
                    if not last_g(g):
                        if p == 0:
                            c_xnT_evac(g + 1)
                        if p == 1:
                            c_qT_evac(g + 1)
                        if p == 2:
                            c_softmax(g + 1)
                        if p == 6:
                            c_x4T_evac(g + 1, 1 - u)

            c_xnT_evac(0)
            c_qT_evac(0)
            c_softmax(0)
            c_x4T_evac(0, 0)
            phase_c(act, c_body)
            t_acc_evac(NG - 1)

        @block.tensor
        def _(pe):
            pe.wait_ge(w_a, 16 * len(A_WEIGHTS))
            pe.wait_ge(cast_done, 1)
            pe.wait_ge(ones_done, 1)

            def turn(dst, src, rows, n, signal):
                for j in range(G):
                    i = pe.transpose(dst[0:n, j * rows:(j + 1) * rows], tile(src, j, n), IDENT[0:rows, 0:rows])
                i.then_inc(signal, 1)

            def a_body(f, g, l, u):
                if f is not None:
                    pe.wait_ge(c_in[u], 16 * (half(f) + 1))
                    turn(bank(0, KW), ctx_rows[u], KEYS, P, a_ctxT_ps)
                if g is not None:
                    pe.wait_ge(a_qT, g + 1)
                    if not first(g):
                        pe.wait_ge(a_x1, g)
                    for j in range(G):
                        i = pe.matmul(tile(bank(1, KW), j, KEYS), tile(qT, j), tile(ctxT[1 - u], j, KEYS),
                                      start=True, stop=True)
                    i.then_inc(a_s_ps, 1)
                if l is not None:
                    pe.wait_ge(a_xn2, l + 1)
                    turn(bank(4), xn2, P, P, a_x2T_ps)
                if f is not None:
                    pe.wait_ge(a_ctxT, f + 1)
                    pe.matmul(bank(2, KW), WK[:, :], ctxT[u], start=True, stop=True).then_inc(a_k_ps, 1)
                    if not first(f):
                        pe.wait_ge(a_v, f)
                    for j in range(G):
                        i = pe.matmul(tile(bank(3, W, KEYS), j), tile(ctxT[u], j, KEYS), WV[:, :],
                                      start=True, stop=True)
                    i.then_inc(a_v_ps, 1)
                    pe.wait_ge(a_xn, f + 1)
                    turn(bank(5), xn, P, P, a_xnT_ps)
                if g is not None:
                    pe.wait_ge(a_exp, g + 1)
                    turn(bank(6, W, KEYS), prob, P, KEYS, a_pT_ps)
                if f is not None:
                    pe.wait_ge(a_xnT, f + 1)
                    pe.matmul(bank(7), W0T[:, :], xnT, start=True, stop=True).then_inc(a_qT_ps, 1)
                if g is not None:
                    pe.wait_ge(a_pT, g + 1)
                    for j in range(G):
                        i = pe.matmul(tile(bank(1), j), tile(probT, j), tile(ctx_rows[1 - u], j),
                                      start=True, stop=True)
                    i.then_inc(a_pv_ps, 1)
                if l is not None:
                    pe.wait_ge(a_x2T, l + 1)
                    if f is not None:
                        pe.wait_ge(a_k, f + 1)
                    for j in range(G):
                        i = pe.matmul(tile(bank(2, G * E), j, E), tile(xn2T_s, j), GATE[:, :], start=True, stop=True)
                    i.then_inc(a_lg_ps, 1)

            phase_a(pe, a_body)

            pe.wait_ge(r_oh, 1)
            pe.matmul(bank(0), before[:, :], onehot_b, start=True, stop=True)
            pe.matmul(bank(1), all_ones[:, :], onehot_b, start=True, stop=True).then_inc(r_cnt, 1)

            pe.wait_ge(a_copied, NG)
            pe.wait_ge(routed, 1)

            def s_gate_up(g):
                for c in range(FC):
                    if not first(g):
                        pe.wait_ge(s_act_d, FC * (g - 1) + c + 1)
                    moving = cols(XN2T, g * W, W)
                    pe.matmul(bank(2 * c), SGU[:, c * P:(c + 1) * P], moving, start=True, stop=True)
                    pe.matmul(bank(2 * c + 1), SGU[:, FI + c * P:FI + (c + 1) * P], moving,
                              start=True, stop=True).then_inc(s_gu_ps, 1)

            def s_down(g, u):
                pe.wait_ge(s_act_d, FC * g + FC)
                if not (isinstance(g, int) and g < 2):
                    pe.wait_ge(s_add, g - 1)
                for j in range(G):
                    for c in range(FC):
                        i = pe.matmul(tile(bank(4 + u), j), s_act[u][:, c * W + j * P:c * W + (j + 1) * P],
                                      SD[:, c * P:(c + 1) * P], start=(c == 0), stop=(c == FC - 1))
                i.then_inc(s_y_ps, 1)

            s_gate_up(0)
            s_gate_up(1)
            s_down(0, 0)
            s_gate_up(2)
            s_down(1, 1)
            with pe.Fori(1, NG // 2 - 1) as i:
                for u in range(2):
                    s_gate_up(2 * i + u + 1)
                    s_down(2 * i + u, u)
            s_gate_up(NG - 1)
            s_down(NG - 2, 0)
            s_down(NG - 1, 1)

            pe.wait_ge(w_exp, 48)
            pe.wait_ge(s_add, NG)

            def r_turn(r, u):
                pe.wait_ge(r_in[u], 16 * (half(r) + 1))
                turn(bank(0), xs_in[u], P, P, r_xT_ps)

            def r_gate_up(q, v, r, u):
                pe.wait_ge(r_xT, r + 1)
                if not (isinstance(q, int) and q < 2):
                    pe.wait_ge(r_act, q - 1)
                for t in range(2):
                    expert = pe.value_load(cols(EXPERT, 2 * q + t, 1)[0:1, :], min_val=0, max_val=E - 1)
                    i = pe.matmul(bank(1 + 2 * v + t), tile(xsT[u], 2 * v + t), cols(WGU, expert * (2 * FI), 2 * FI),
                                  start=True, stop=True)
                i.then_inc(r_gu_ps, 1)

            def r_turn_act(q, v):
                pe.wait_ge(r_act, q + 1)
                if not first(q):
                    pe.wait_ge(r_aT, q)
                turn(bank(5), ract[v], P, P, r_aT_ps)

            def r_down(q, v, u):
                pe.wait_ge(r_aT, q + 1)
                for t in range(2):
                    expert = pe.value_load(cols(EXPERT, 2 * q + t, 1)[0:1, :], min_val=0, max_val=E - 1)
                    for c in range(FC):
                        i = pe.matmul(tile(bank(6 + u), 2 * v + t), tile(actT[v], 2 * t + c),
                                      cols(WD, expert * (FC * P) + c * P, P), start=(c == 0), stop=(c == FC - 1))
                i.then_inc(r_y_ps, 1)

            def r_body(r, u):
                if not last_r(r):
                    r_turn(r + 1, 1 - u)
                q = 2 * r
                r_gate_up(q + 1, 1, r, u)
                r_turn_act(q, 0)
                if not first(r):
                    r_down(q - 1, 1, 1 - u)
                if not last_r(r):
                    r_gate_up(q + 2, 0, r + 1, 1 - u)
                r_turn_act(q + 1, 1)
                if not (isinstance(r, int) and r < 2):
                    pe.wait_ge(r_y, r - 1)
                r_down(q, 0, u)

            r_turn(0, 0)
            r_gate_up(0, 0, 0, 0)
            r_body(0, 0)
            r_body(1, 1)
            r_body(2, 0)
            with pe.Fori(1, NR // 2 - 1) as i:
                r_body(2 * i + 1, 1)
                r_body(2 * i + 2, 0)
            r_body(NR - 1, 1)
            r_down(2 * NR - 1, 1, 1)

            def c_turn_x(h):
                pe.wait_ge(c_xn3, h + 1)
                turn(bank(5), xn3, P, P, c_xnT_ps)

            def c_query(h):
                pe.wait_ge(c_xnT, h + 1)
                pe.matmul(bank(6), WQ[:, :], xn3T, start=True, stop=True).then_inc(c_qT_ps, 1)

            def c_scores(h):
                pe.wait_ge(c_qT, h + 1)
                if not first(h):
                    if not (isinstance(h, int) and h == 1):
                        pe.wait_ge(t_res, h - 1)
                for j in range(G):
                    i = pe.matmul(tile(bank(7, KW), j, KEYS), tile(q1T, j), cols(KT, h * KW + j * KEYS, KEYS),
                                  start=True, stop=True)
                i.then_inc(c_s_ps, 1)

            def c_turn_prob(h):
                pe.wait_ge(c_exp, h + 1)
                turn(bank(5, W, KEYS), prob1, P, KEYS, c_pT_ps)

            def c_values(h):
                pe.wait_ge(c_pT, h + 1)
                for j in range(G):
                    i = pe.matmul(tile(bank(6), j), tile(prob1T, j), cols(V, h * W + j * P, P), start=True, stop=True)
                i.then_inc(c_pv_ps, 1)

            def c_turn_x4(h):
                pe.wait_ge(c_xn4, h + 1)
                turn(bank(7), xn3, P, P, c_x4T_ps)

            def t_logits(g, p, u):
                q = TREES * g + p
                pe.wait_ge(c_x4T, g + 1)
                if not (isinstance(q, int) and q < 2):
                    pe.wait_ge(t_sil, q - 1)
                for c in range(2):
                    i = pe.matmul(bank(2 * (p % 2) + c), tile(WIN, 2 * p + c), x4T[u], start=True, stop=(c == 1),
                                  skip_group_check=True)
                    if c == 0:
                        i.then_inc(t_in, 1)

            def t_path(g, p):
                q = TREES * g + p
                pe.wait_ge(t_dec, q + 1)
                pe.matmul(bank(2 * (p % 2)), anc_in[:, :], dec[p % 2], start=False, stop=True, skip_group_check=True)
                pe.matmul(bank(2 * (p % 2) + 1), anc_lv[:, :], dec[p % 2], start=False, stop=True,
                          skip_group_check=True).then_inc(t_mask, 1)

            def t_output(g, p):
                q = TREES * g + p
                pe.wait_ge(t_sil, q + 1)
                if p == 0 and not first(g):
                    pe.wait_ge(t_accT, g)
                for c in range(2):
                    i = pe.matmul(bank(4), tile(WOUT, 2 * p + c), tile(sil[p % 2], c, W),
                                  start=(p == 0 and c == 0), stop=(p == TREES - 1 and c == 1))
                i.then_inc(t_out, 1)

            def c_body(g, u):
                for p in range(TREES):
                    if p + 1 < TREES:
                        t_logits(g, p + 1, u)
                    elif not last_g(g):
                        t_logits(g + 1, 0, 1 - u)
                    t_path(g, p)
                    if p:
                        t_output(g, p - 1)
                    elif not first(g):
                        t_output(g - 1, TREES - 1)
                    if p == 1 and not first(g):
                        pe.wait_ge(t_accT, g)
                        turn(bank(7), accT, P, P, t_acc)
                    if not last_g(g):
                        if p == 0:
                            c_turn_x(g + 1)
                        if p == 1:
                            c_query(g + 1)
                        if p == 2:
                            c_scores(g + 1)
                        if p == 3:
                            c_turn_prob(g + 1)
                        if p == 4:
                            c_values(g + 1)
                        if p == 6:
                            c_turn_x4(g + 1)

            c_turn_x(0)
            c_query(0)
            c_scores(0)
            c_turn_prob(0)
            c_values(0)
            c_turn_x4(0)
            t_logits(0, 0, 0)
            phase_c(pe, c_body)
            t_output(NG - 1, TREES - 1)
            pe.wait_ge(t_accT, NG)
            turn(bank(7), accT, P, P, t_acc)

        @block.vector
        def _(dve):
            dve.wait_ge(w_a, 16 * len(A_WEIGHTS))
            dve.tensor_copy(anc_in[:, :], WA[:, C_IN:C_IN + P])
            dve.tensor_copy(anc_lv[:, :], WA[:, C_LV:C_LV + P])
            dve.tensor_copy(before[:, :], WA[:, C_BEF:C_BEF + P]).then_inc(cast_done, 1)

            def stats(s, g, st_done, mv_done):
                dve.sem_inc(dve_passed, 1)
                for j in range(G):
                    i = dve.bn_stats(st[:, s, j, :], cols(X, g * W + j * P, P))
                i.then_inc(st_done, 1)
                dve.wait_ge(st_done, g + 1)
                dve.sem_inc(dve_passed, 1)
                for j in range(G):
                    i = dve.bn_aggr(mv[:, s, j, :], st[:, s, j, :])
                i.then_inc(mv_done, 1)

            def normalise(s, g, rs_done, dst, done):
                dve.wait_ge(rs_done, g + 1)
                for j in range(G):
                    i = dve.tensor_scalar(tile(dst, j), cols(X, g * W + j * P, P), mv[:, s, j, 0:1],
                                          rs[:, s, j:j + 1], ALU.subtract, ALU.mult)
                i.then_inc(done, 1)

            def a_body(f, g, l, u):
                if f is not None:
                    dve.wait_ge(x_in[u], 16 * (half(f) + 1))
                    stats(0, f, a_st1, a_mv1)
                if g is not None:
                    dve.wait_ge(a_s_ps, g + 1)
                    dve.tensor_reduce(nmax[:, :], by_tile(bank(1, KW), KEYS), AX.X, ALU.max,
                                      negate=True).then_inc(a_max, 1)
                if f is not None:
                    if not first(f):
                        dve.wait_ge(a_xnT_ps, f)
                    normalise(0, f, a_rs1, xn, a_xn)
                    dve.wait_ge(a_v_ps, f + 1)
                    dve.tensor_tensor(by_tile(cols(V, f * W, W)), by_tile(bank(3, W, KEYS)),
                                      bvr[:, :].unsqueeze(1).to_broadcast([KEYS, G, P]), ALU.add).then_inc(a_v, 1)
                if g is not None:
                    dve.wait_ge(a_pT_ps, g + 1)
                    dve.tensor_copy(probT, bank(6, W, KEYS)).then_inc(a_pT, 1)
                    dve.wait_ge(a_exp, g + 1)
                    dve.reciprocal(srec[:, :], ssum[:, :]).then_inc(a_rec, 1)
                    dve.wait_ge(a_rec, g + 1)
                    dve.wait_ge(a_pv_ps, g + 1)
                    for j in range(G):
                        row = cols(X, g * W + j * P, P)
                        i = dve.scalar_tensor_tensor(out=row, in0=tile(bank(1), j), scalar=srec[:, j:j + 1],
                                                     in1=row, op0=ALU.mult, op1=ALU.add)
                    i.then_inc(a_x1, 1)
                    dve.wait_ge(a_x1, g + 1)
                    if not first(g):
                        dve.wait_ge(a_mean, g)
                    stats(1, g, a_st2, a_mv2)
                if l is not None:
                    dve.wait_ge(a_lg_ps, l + 1)
                    dve.tensor_copy(cols(LG, l * (G * E), G * E), bank(2, G * E)).then_inc(a_lg, 1)
                if g is not None:
                    if not first(g):
                        dve.wait_ge(a_x2T_ps, g)
                    normalise(1, g, a_rs2, xn2, a_xn2)

            phase_a(dve, a_body)

            steps = [0]

            def step(ins):
                steps[0] += 1
                ins.then_inc(route, 1)
                dve.wait_ge(route, steps[0])

            def te(a):
                return a.rearrange("p (t e) -> p t e", e=E)

            def et(a):
                return a.rearrange("p (e t) -> p e t", e=E)

            def over_e(a, n=B):
                return a.unsqueeze(2).to_broadcast([P, n, E])

            dve.wait_ge(a_lg, NG)
            dve.wait_ge(a_mean, NG)
            rank = c_rout[:, 0:E]
            tile_no = c_rout[:, E:E + SLOT_TILES]
            keep = c_rout[:, E + SLOT_TILES:]
            dve.tensor_reduce(top, te(LG[:, :]), AX.X, ALU.max).then_inc(top_done, 1)
            dve.wait_ge(top_done, 1)
            step(dve.tensor_tensor(te(lead), te(LG[:, :]), over_e(top), ALU.is_ge))
            step(dve.tensor_tensor(te(lead), te(lead), rank.unsqueeze(1).to_broadcast([P, B, E]), ALU.mult))
            step(dve.tensor_reduce(best, te(lead), AX.X, ALU.max))
            step(dve.tensor_tensor(te(onehot), te(lead), over_e(best), ALU.is_equal))
            dve.tensor_copy(onehot_b, onehot).then_inc(r_oh, 1)
            dve.wait_ge(r_cnt, 1)
            step(dve.tensor_copy(et(counts), bank(1).rearrange("p (t e) -> p e t", e=E)))
            step(dve.tensor_tensor_scan(upto, keep, counts, 0.0, ALU.mult, ALU.add))
            step(dve.tensor_scalar(tiles_i, et(upto)[:, :, B - 1], float(P - 1), None, ALU.add))
            step(dve.tensor_scalar(tiles_i, tiles_i, 7, None, ALU.logical_shift_right))
            step(dve.tensor_copy(tiles_f, tiles_i))
            step(dve.tensor_tensor_scan(tile_end, keep[:, 1:1 + E], tiles_f, 0.0, ALU.mult, ALU.add))
            step(dve.tensor_tensor(first_slot, tile_end, tiles_f, ALU.subtract))
            step(dve.tensor_scalar(first_slot, first_slot, float(P), None, ALU.mult))
            step(dve.tensor_tensor(slot, upto, counts, ALU.subtract))
            step(dve.tensor_tensor(et(slot), et(slot), first_slot.unsqueeze(2).to_broadcast([P, E, B]), ALU.add))
            step(dve.tensor_tensor(te(lead), te(bank(0)), slot.rearrange("p (e t) -> p t e", e=E), ALU.add))
            step(dve.tensor_tensor(lead, lead, onehot, ALU.mult))
            step(dve.tensor_reduce(posf, te(lead), AX.X, ALU.add))
            step(dve.tensor_copy(POS[:, :], posf))
            step(dve.tensor_tensor(te(passed), over_e(tile_no, SLOT_TILES),
                                   tile_end.unsqueeze(1).to_broadcast([P, SLOT_TILES, E]), ALU.is_ge))
            step(dve.tensor_reduce(expert_f, te(passed), AX.X, ALU.add))
            step(dve.tensor_scalar(EXPERT[:, :], expert_f, float(E - 1), None, ALU.min))
            dve.wait_ge(scored, 1)
            step(dve.tensor_tensor(RSTD2[:, :], RSTD2[:, :], score, ALU.mult))
            dve.sem_inc(routed, 1)
            dve.sem_inc(pos_done, 1)

            def s_body(g, u):
                if not (isinstance(g, int) and g < 2):
                    dve.wait_ge(scattered, 16 * G * (g - 1))
                for j in range(G):
                    i = dve.tensor_scalar(tile(xs[u], j), cols(X, g * W + j * P, P), cols(MEAN2, g * G + j, 1),
                                          cols(RSTD2, g * G + j, 1), ALU.subtract, ALU.mult)
                i.then_inc(s_xs, 1)
                for c in range(FC):
                    dve.wait_ge(s_sil, FC * g + c + 1)
                    a = tile(s_act[u], c, W)
                    dve.tensor_tensor(a, a, bank(2 * c + 1), ALU.mult).then_inc(s_act_d, 1)
                dve.wait_ge(s_y_ps, g + 1)
                row = cols(X, g * W, W)
                dve.tensor_tensor(row, row, bank(4 + u), ALU.add).then_inc(s_add, 1)

            s_body(0, 0)
            s_body(1, 1)
            with dve.Fori(1, NG // 2) as i:
                for u in range(2):
                    s_body(2 * i + u, u)

            def r_mul(q, v):
                dve.wait_ge(r_sg, q + 1)
                if not (isinstance(q, int) and q < 2):
                    dve.wait_ge(r_aT_ps, q - 1)
                pair = by_tile(PS[:, 512 * (1 + 2 * v):512 * (3 + 2 * v)], 512)
                dve.tensor_tensor(by_tile(ract[v], FI), by_tile(sg[v], FI), pair[:, :, FI:], ALU.mult).then_inc(r_act, 1)

            def r_evac_a(q, v):
                dve.wait_ge(r_aT_ps, q + 1)
                if not (isinstance(q, int) and q < 2):
                    dve.wait_ge(r_y_ps, q - 1)
                dve.tensor_copy(actT[v], bank(5)).then_inc(r_aT, 1)

            r_mul(0, 0)
            r_mul(1, 1)
            r_evac_a(0, 0)
            r_mul(2, 0)
            r_evac_a(1, 1)
            with dve.Fori(1, NR - 1) as r:
                r_mul(2 * r + 1, 1)
                r_evac_a(2 * r, 0)
                r_mul(2 * r + 2, 0)
                r_evac_a(2 * r + 1, 1)
            r_mul(2 * NR - 1, 1)
            r_evac_a(2 * NR - 2, 0)
            r_evac_a(2 * NR - 1, 1)

            def c_front(h, u):
                dve.wait_ge(y_in[u], 16 * G * (half(h) + 1))
                row = cols(X, h * W, W)
                dve.tensor_tensor(row, row, ys[u], ALU.add).then_inc(c_x2, 1)
                dve.wait_ge(c_x2, h + 1)
                stats(0, h, c_st3, c_mv3)
                if not first(h):
                    dve.wait_ge(c_x4T_ps, h)
                normalise(0, h, c_rs3, xn3, c_xn3)

            def c_max_scores(h):
                dve.wait_ge(c_s_ps, h + 1)
                dve.tensor_reduce(nmax[:, :], by_tile(bank(7, KW), KEYS), AX.X, ALU.max, negate=True).then_inc(c_max, 1)
                dve.wait_ge(c_max, h + 1)
                dve.tensor_scalar(nmax_s[:, :], nmax[:, :], SCALE, None, ALU.mult).then_inc(c_maxs, 1)

            def c_evac_prob(h):
                dve.wait_ge(c_pT_ps, h + 1)
                dve.tensor_copy(prob1T, bank(5, W, KEYS)).then_inc(c_pT, 1)
                dve.wait_ge(c_exp, h + 1)
                dve.reciprocal(srec[:, :], ssum[:, :]).then_inc(c_rec, 1)

            def c_attended(h):
                dve.wait_ge(c_rec, h + 1)
                dve.wait_ge(c_pv_ps, h + 1)
                for j in range(G):
                    row = cols(X, h * W + j * P, P)
                    i = dve.scalar_tensor_tensor(out=row, in0=tile(bank(6), j), scalar=srec[:, j:j + 1],
                                                 in1=row, op0=ALU.mult, op1=ALU.add)
                i.then_inc(c_x3, 1)
                dve.wait_ge(c_x3, h + 1)
                stats(1, h, c_st4, c_mv4)

            def c_norm4(h):
                normalise(1, h, c_rs4, xn3, c_xn4)

            def t_decide(g, p):
                q = TREES * g + p
                dve.wait_ge(t_in, q + 1)
                if not (isinstance(q, int) and q < 2):
                    dve.wait_ge(t_mask, q - 1)
                dve.tensor_scalar(dec[p % 2], bank(2 * (p % 2)), b_in_c[:, 2 * p:2 * p + 1], 0.0,
                                  ALU.add, ALU.is_gt).then_inc(t_dec, 1)

            def t_result(g, u, stores):
                dve.wait_ge(t_acc, g + 1)
                dve.wait_ge(stored[u], 16 * (stores + 1))
                dve.tensor_tensor(res[u], cols(X, g * W, W), bank(7), ALU.add).then_inc(t_res, 1)

            def c_body(g, u, stores):
                for p in range(TREES):
                    t_decide(g, p)
                    if p == 1 and not first(g):
                        t_result(g - 1, 1 - u, stores)
                    if not last_g(g):
                        if p == 0:
                            c_front(g + 1, 1 - u)
                        if p == 3:
                            c_max_scores(g + 1)
                        if p == 4:
                            c_evac_prob(g + 1)
                        if p == 5:
                            c_attended(g + 1)
                        if p == 6:
                            c_norm4(g + 1)

            c_front(0, 0)
            c_max_scores(0)
            c_evac_prob(0)
            c_attended(0)
            c_norm4(0)
            c_body(0, 0, None)
            with dve.Fori(0, NG // 2 - 1) as i:
                c_body(2 * i + 1, 1, i)
                c_body(2 * i + 2, 0, i)
            c_body(NG - 1, 1, NG // 2 - 1)
            t_result(NG - 1, 1, NG // 2 - 1)


_OUT = (B, P, P)


def kernel(**inputs):
    import concourse.bacc as bacc
    from concourse.bass_utils import run_bass_kernel_spmd

    a = {k: np.ascontiguousarray(v) for k, v in inputs.items()}
    nodes = 2 * P - 1

    def by_chunk(w, last):
        w = w.reshape(TREES, nodes, -1)
        pad = np.full((TREES, 1, w.shape[2]), last, w.dtype)
        return np.concatenate([w[:, :P - 1], pad, w[:, P - 1:]], 1).reshape(TREES * 2 * P, -1)

    arrays = {
        "x": a["x"], "ctx_kv": a["ctx_1024"], "w0": np.ascontiguousarray(a["L0_xattn_W"].T), "b0": a["L0_xattn_b"],
        "gate": a["L0_ffn_gate_w"], "sh_gate": a["L0_ffn_sh_gate"], "sh_up": a["L0_ffn_sh_up"],
        "sh_down": a["L0_ffn_sh_down"], "rt_gate": a["L0_ffn_rt_gate"], "rt_up": a["L0_ffn_rt_up"],
        "rt_down": a["L0_ffn_rt_down"], "wq": a["L1_xattn_Wq"], "bq": a["L1_xattn_bq"], "wk": a["L1_xattn_Wk"],
        "bk": a["L1_xattn_bk"], "wv": a["L1_xattn_Wv"], "bv": a["L1_xattn_bv"],
        "w_in": np.ascontiguousarray(by_chunk(a["L1_ffn_W_in"], 0.0).T),
        "b_in": np.ascontiguousarray(by_chunk(a["L1_ffn_b_in"], 1.0).reshape(2 * TREES, P).T),
        "w_out": by_chunk(np.ascontiguousarray(a["L1_ffn_W_out"].T), 0.0),
        "const": constants(),
    }
    nc = bacc.Bacc("TRN2", target_bir_lowering=False, num_devices=1)
    args = [nc.dram_tensor(f"in_{k}", v.shape, mybir.dt.from_np(v.dtype), kind="ExternalInput").ap()
            for k, v in arrays.items()]
    out = nc.dram_tensor("out_0", _OUT, F32, kind="ExternalOutput").ap()
    program(nc, *args, out)
    r = run_bass_kernel_spmd(nc, [{f"in_{k}": v for k, v in arrays.items()}], core_ids=[0])
    return r.results[0]["out_0"]
```

```python
from contextlib import ExitStack

import numpy as np

import concourse.bass as bass
from concourse import mybir

F32 = mybir.dt.float32
F32R = mybir.dt.float32r
BF16 = mybir.dt.bfloat16
I32 = mybir.dt.int32
ALU = mybir.AluOpType
ACT = mybir.ActivationFunctionType
AX = mybir.AxisListType

P = 128
B = 64
KEYS = 120
G = 4
NG = B // G
W = G * P
KW = G * KEYS
E = 8
FI = 256
FC = FI // P
HALVES = 2
HB = B // HALVES
HG = NG // HALVES
HTILES = HB + E
SLOT_TILES = HALVES * HTILES
NR = SLOT_TILES // G
ZERO_PARTS = 5
HR = NR // HALVES
TREES = 8
DEPTH = 7
BIG = float(2.0 ** 40)
EPS = 1e-5
SCALE = float(P) ** -0.5


def constants():
    ident = np.eye(P, dtype=np.float32)
    inner = np.zeros((P, P), np.float32)
    leaves = np.zeros((P, P), np.float32)
    for node in range(2 * P - 1):
        table, col = (inner, node) if node < P - 1 else (leaves, node - (P - 1))
        child = node
        while child > 0:
            parent = (child - 1) // 2
            if child == 2 * parent + 2:
                table[parent, col] += BIG
                table[P - 1, col] -= BIG
            else:
                table[parent, col] -= BIG
            child = parent
    before = np.triu(np.ones((P, P), np.float32), 1)
    rank = np.broadcast_to(np.arange(E, 0, -1, dtype=np.float32), (P, E))
    tile = np.broadcast_to(np.arange(HTILES, dtype=np.float32), (P, HTILES))
    keep = np.ones((P, E, HB), np.float32)
    keep[:, :, 0] = 0.0
    return np.ascontiguousarray(np.concatenate([ident, inner, leaves, before, rank, tile, keep.reshape(P, E * HB)], 1))


C_ID, C_IN, C_LV, C_BEF = 0, P, 2 * P, 3 * P
C_RANK = 4 * P
C_TILE = C_RANK + E
C_KEEP = C_TILE + HTILES
C_END = C_KEEP + E * HB


def program(nc, x, ctx_kv, w0, b0, gate, sh_gate, sh_up, sh_down, rt_gate, rt_up, rt_down,
            wq, bq, wk, bk, wv, bv, w_in, b_in, w_out, const, out):
    x_sorted = nc.dram_tensor("x_sorted", (SLOT_TILES * P, P), F32, kind="Internal").ap()
    rows2 = nc.dram_tensor("rows2", (B, P, P), F32, kind="Internal").ap()
    y_sorted = nc.dram_tensor("y_sorted", (SLOT_TILES * P, P), F32, kind="Internal").ap()
    with ExitStack() as ctx:
        def sb(name, shape, dt=F32):
            return ctx.enter_context(nc.sbuf_tensor(name, shape, dt))

        def sem(name):
            return ctx.enter_context(nc.semaphore(name))

        def sems(name, n):
            return [sem(f"{name}{i}") for i in range(n)]

        X = sb("X", [P, B * P])
        KT = sb("KT", [P, B * KEYS])
        V = sb("V", [KEYS, B * P])
        WA = sb("WA", [P, C_RANK])
        c_rout = sb("c_rout", [P, C_END - C_RANK])
        anc_in = sb("anc_in", [P, P], BF16)
        anc_lv = sb("anc_lv", [P, P], BF16)
        before = sb("before", [P, P], BF16)
        all_ones = sb("all_ones", [P, P], BF16)
        W0T = sb("W0T", [P, P])
        WQ = sb("WQ", [P, P])
        WK = sb("WK", [P, P])
        WV = sb("WV", [P, P])
        GATE = sb("GATE", [P, E])
        SGU = sb("SGU", [P, 2 * FI])
        SD = sb("SD", [P, FC * P])
        b_in_c = sb("b_in_c", [P, 2 * TREES])
        b0c = sb("b0c", [P, 1])
        bqc = sb("bqc", [P, 1])
        bkc = sb("bkc", [P, 1])
        bvr = sb("bvr", [KEYS, P])
        neg_half = sb("neg_half", [P, G])
        eps = sb("eps", [P, G])
        SCORE = sb("SCORE", [P, B])
        POS = sb("POS", [P, B], I32)
        EXPERT = sb("EXPERT", [P, SLOT_TILES], I32)
        LG = sb("LG", [P, HB * E])
        st = sb("st", [P, 2, G, 6])
        mv = sb("mv", [P, 2, G, 2])
        ve = sb("ve", [P, 2, G])
        rs = sb("rs", [P, 2, G])
        nmax = sb("nmax", [P, G])
        nmax_s = sb("nmax_s", [P, G])
        ssum = sb("ssum", [P, G])
        srec = sb("srec", [P, G])
        idx = sb("idx", [P, 2, G], I32)
        sco = sb("sco", [P, 2, G])
        PS = ctx.enter_context(nc.psum_tensor("PS", [P, 8 * 512], F32))

        TREE_W, EXPERT_W = 4 * 2 * TREES * P, E * 2 * FI + E * FC * P
        WORK = TREE_W + EXPERT_W
        ARENA = WORK + 10240
        arena_base = -(-nc.sbuf_base // 32) * 32
        ctx.enter_context(nc.sbuf_tensor("arena", [P, ARENA + 8], F32))

        class Cut:
            def __init__(self, start, end):
                self.at, self.end = start, end

            def take(self, name, n, parts=P, dt=F32):
                size = n if dt != BF16 else n // 2
                t = nc.alloc_sbuf_tensor_at(name, [parts, n], dt, offset=arena_base + 4 * self.at)
                self.at += size
                assert self.at <= self.end, name
                return t[:, :]

            def two(self, name, n, parts=P, dt=F32):
                return [self.take(f"{name}{i}", n, parts, dt) for i in range(2)]

        def bank(i, n=512, parts=P):
            return PS[0:parts, 512 * i:512 * i + n]

        IDENT = WA[:, C_ID:C_ID + P]
        NODES = 2 * TREES * P
        cut = Cut(0, TREE_W)
        win_h, win_l, wout_h, wout_l = (cut.take(n, NODES, dt=F32R) for n in ("win_h", "win_l", "wout_h", "wout_l"))
        cut = Cut(TREE_W, WORK)
        win_f, wout_f = cut.take("win_f", NODES), cut.take("wout_f", NODES)
        cut = Cut(TREE_W, WORK)
        WGU = cut.take("WGU", E * 2 * FI)
        WD = cut.take("WD", E * FC * P)
        cut = Cut(WORK, ARENA)
        xs = cut.two("xs", W)
        scatter_end = cut.at
        ctx_rows = cut.two("ctx_rows", W, KEYS)
        ctxT = cut.two("ctxT", KW)
        xn = cut.take("xn", W)
        xnT = cut.take("xnT", W)
        qT = cut.take("qT", W)
        prob = cut.take("prob", KW)
        probT = cut.take("probT", W, KEYS)
        xn2 = cut.take("xn2", W)
        xn2T = cut.take("xn2T", W)
        s_act = cut.take("s_act", FC * W)
        zeros = cut.take("zeros", P)
        lead = cut.take("lead", HB * E)
        onehot = cut.take("onehot", HB * E)
        slot = cut.take("slot", HB * E)
        counts = cut.take("counts", HB * E)
        upto = cut.take("upto", HB * E)
        top = cut.take("top", HB)
        best = cut.take("best", HB)
        posf = cut.take("posf", HB)
        tiles_i = cut.take("tiles_i", E, dt=I32)
        tiles_f = cut.take("tiles_f", E)
        tile_end = cut.take("tile_end", E)
        first_slot = cut.take("first_slot", E)
        passed = cut.take("passed", HTILES * E)
        expert_f = cut.take("expert_f", HTILES)
        onehot_b = cut.take("onehot_b", HB * E, dt=BF16)
        cut = Cut(scatter_end, ARENA)
        xs_in = cut.two("xs_in", W)
        xsT = cut.two("xsT", W)
        sg = cut.two("sg", 2 * FI)
        ract = cut.two("ract", 2 * FI)
        actT = cut.two("actT", 2 * FI)
        yo = cut.two("yo", W)
        cut = Cut(TREE_W, ARENA)
        sil_h = cut.two("sil_h", 2 * W, dt=F32R)
        sil_l = cut.two("sil_l", 2 * W, dt=F32R)
        sil = cut.two("sil", 2 * W)
        x4T_h = cut.take("x4T_h", W, dt=F32R)
        x4T_l = cut.take("x4T_l", W, dt=F32R)
        ys = cut.two("ys", W)
        xn3 = cut.take("xn3", W)
        xn4 = cut.take("xn4", W)
        xn3T = cut.take("xn3T", W)
        q1T = cut.take("q1T", W)
        prob1 = cut.take("prob1", KW)
        prob1T = cut.take("prob1T", W, KEYS)
        accT = cut.take("accT", W)
        dec = cut.two("dec", W, dt=BF16)
        res = cut.two("res", W)

        x_in, c_in, w_a, w_tree, w_exp = sems("x_in", 2), sems("c_in", 2), sem("w_a"), sem("w_tree"), sem("w_exp")
        cast_done, zero_done, zeroed, half_done, ones_done, tree_hi, tree_split = (
            sem(n) for n in ("cast_done", "zero_done", "zeroed", "half_done", "ones_done", "tree_hi", "tree_split"))
        (a_ctxT_ps, a_ctxT, a_k_ps, a_k, a_v_ps, a_v, a_st1, a_mv1, a_ve1, a_rs1, a_xn, a_xnT_ps, a_xnT, a_qT_ps, a_qT,
         a_s_ps, a_max, a_exp, a_pT_ps, a_pT, a_pv_ps, a_rec, a_x1, a_st2, a_mv2, a_ve2, a_rs2, a_xn2, a_rows,
         a_x2T_ps, a_x2T, a_lg_ps, a_lg) = (sem(n) for n in (
             "a_ctxT_ps", "a_ctxT", "a_k_ps", "a_k", "a_v_ps", "a_v", "a_st1", "a_mv1", "a_ve1", "a_rs1", "a_xn",
             "a_xnT_ps", "a_xnT", "a_qT_ps", "a_qT", "a_s_ps", "a_max", "a_exp", "a_pT_ps", "a_pT", "a_pv_ps", "a_rec",
             "a_x1", "a_st2", "a_mv2", "a_ve2", "a_rs2", "a_xn2", "a_rows", "a_x2T_ps", "a_x2T", "a_lg_ps", "a_lg"))
        s_gu_ps, s_sil, s_act_d, s_y_ps, s_add = (sem(n) for n in ("s_gu_ps", "s_sil", "s_act_d", "s_y_ps", "s_add"))
        top_done, route, r_oh, r_cnt, scored, routed, dve_passed, pool_passed = (
            sem(n) for n in ("top_done", "route", "r_oh", "r_cnt", "scored", "routed", "dve_passed", "pool_passed"))
        k_idx, k_scaled, k_in, scattered = sem("k_idx"), sem("k_scaled"), sems("k_in", 2), sems("scattered", 2)
        r_in, r_out = sems("r_in", 2), sems("r_out", 2)
        r_xT_ps, r_xT, r_gu_ps, r_sg, r_act, r_aT_ps, r_aT, r_y_ps, r_y = (sem(n) for n in (
            "r_xT_ps", "r_xT", "r_gu_ps", "r_sg", "r_act", "r_aT_ps", "r_aT", "r_y_ps", "r_y"))
        y_in, stored = sems("y_in", 2), sems("stored", 2)
        (c_idx, c_x2, c_st3, c_mv3, c_ve3, c_rs3, c_xn3, c_xnT_ps, c_xnT, c_qT_ps, c_qT, c_s_ps, c_max, c_maxs, c_exp,
         c_pT_ps, c_pT, c_pv_ps, c_rec, c_x3, c_st4, c_mv4, c_ve4, c_rs4, c_xn4, c_x4T_ps, c_x4h, c_x4l) = (
             sem(n) for n in (
                 "c_idx", "c_x2", "c_st3", "c_mv3", "c_ve3", "c_rs3", "c_xn3", "c_xnT_ps", "c_xnT", "c_qT_ps", "c_qT",
                 "c_s_ps", "c_max", "c_maxs", "c_exp", "c_pT_ps", "c_pT", "c_pv_ps", "c_rec", "c_x3", "c_st4", "c_mv4",
                 "c_ve4", "c_rs4", "c_xn4", "c_x4T_ps", "c_x4h", "c_x4l"))
        t_in, t_dec, t_mask, t_silu, t_hi, t_hi_dve, t_lo, t_out, t_acc, t_accT, t_res = (sem(n) for n in (
            "t_in", "t_dec", "t_mask", "t_silu", "t_hi", "t_hi_dve", "t_lo", "t_out", "t_acc", "t_accT", "t_res"))

        block = ctx.enter_context(nc.Block())

        def cols(a, start, n):
            return a[:, start:start + n] if isinstance(start, int) else a[:, bass.ds(start, n)]

        def tile(a, j, n=P):
            return a[:, j * n:(j + 1) * n]

        def by_tile(a, n=P):
            return a.rearrange("p (t n) -> p t n", n=n)

        def first(g):
            return isinstance(g, int) and g == 0

        def below(g, n):
            return isinstance(g, int) and g < n

        def last(g, n):
            return isinstance(g, int) and g >= NG - n

        def last_unit(r):
            return isinstance(r, int) and r == NR - 1

        DVE_TREE = 1

        def phase_a(eng, body, route):
            body(0, None, None, None, 0, None)
            body(1, 0, None, None, 1, None)
            body(2, 1, 0, None, 0, None)
            with eng.Fori(0, HG // 2 - 1) as i:
                for u in range(2):
                    f = 2 * i + 3 + u
                    body(f, f - 1, f - 2, f - 3, 1 - u, None)
            body(HG + 1, HG, HG - 1, HG - 2, 1, None)
            route(0)
            with eng.Fori(0, HG // 2 - 1) as i:
                for u in range(2):
                    f = 2 * i + HG + 2 + u
                    body(f, f - 1, f - 2, f - 3, u, 2 * i + u)
            body(None, NG - 1, NG - 2, NG - 3, 0, HG - 2)
            body(None, None, NG - 1, NG - 2, 1, HG - 1)
            body(None, None, None, NG - 1, 0, None)

        def phase_c(eng, body):
            body(0, 0, None)
            with eng.Fori(0, NG // 2 - 2) as i:
                body(2 * i + 1, 1, i)
                body(2 * i + 2, 0, i)
            for g in range(NG - 3, NG):
                body(g, g % 2, (g - 1) // 2)

        A_WEIGHTS = [(WA[:, :], const[:, 0:C_RANK]), (W0T[:, :], w0), (b0c[:, :], b0.rearrange("(p a) -> p a", a=1)),
                     (WK[:, :], wk), (bkc[:, :], bk.rearrange("(p a) -> p a", a=1)), (WV[:, :], wv),
                     (bvr[:, :], bv.partition_broadcast(KEYS)), (SGU[:, 0:FI], sh_gate), (SGU[:, FI:], sh_up),
                     (by_tile(SD[:, :]), sh_down.rearrange("(c i) h -> i c h", c=FC)), (GATE[:, :], gate),
                     (WQ[:, :], wq), (bqc[:, :], bq.rearrange("(p a) -> p a", a=1)),
                     (c_rout[:, :], const[:, C_RANK:C_END]), (b_in_c[:, :], b_in)]

        @block.sync
        def _(sp):
            for u in range(2):
                sp.sem_inc(r_out[u], 16)
                sp.sem_inc(stored[u], 16)

            def load_group(g, u):
                sp.dma_start(by_tile(cols(X, g * W, W)),
                             x[bass.ds(g * G, G), :, :].rearrange("b s d -> s b d")).then_inc(x_in[u], 16)
                sp.dma_start(by_tile(ctx_rows[u]),
                             ctx_kv[bass.ds(g * G, G), :, :].rearrange("b s d -> s b d")).then_inc(c_in[u], 16)

            load_group(0, 0)
            load_group(1, 1)
            sp.dma_start(win_f, w_in).then_inc(w_tree, 16)
            sp.dma_start(by_tile(wout_f), w_out.rearrange("(c i) h -> i c h", c=2 * TREES)).then_inc(w_tree, 16)

            def load_experts():
                sp.wait_ge(tree_split, 1)
                gu = WGU.rearrange("p (e n) -> p e n", e=E)
                sp.dma_start(gu[:, :, 0:FI], rt_gate.rearrange("e h i -> h e i")).then_inc(w_exp, 16)
                sp.dma_start(gu[:, :, FI:], rt_up.rearrange("e h i -> h e i")).then_inc(w_exp, 16)
                sp.dma_start(by_tile(WD), rt_down.rearrange("e (c i) h -> i (e c) h", c=FC)).then_inc(w_exp, 16)

            def load_rows(k, v, i):
                if not below(i, 1):
                    sp.wait_ge(scattered[v], 16 * G * i)
                sp.wait_ge(a_rows, 16 * (k + 1))
                sp.dma_start(by_tile(xs[v]), rows2[bass.ds(k * G, G), :, :].rearrange("b s d -> s b d")
                             ).then_inc(k_in[v], 16)

            def a_body(g, v, load):
                if load:
                    sp.wait_ge(a_pv_ps, g + 1)
                    load_group(g + 2, v)
                sp.wait_ge(a_xn2, g + 1)
                sp.dma_start(rows2[bass.ds(g * G, G), :, :].rearrange("b s d -> s b d"),
                             by_tile(xn2)).then_inc(a_rows, 16)

            def zero_slots(part):
                n = SLOT_TILES // ZERO_PARTS
                sp.dma_start(x_sorted[part * n * P:(part + 1) * n * P, :].rearrange("(t p) d -> p t d", p=P),
                             zeros.unsqueeze(1).to_broadcast([P, n, P])).then_inc(zeroed, 16)

            sp.wait_ge(zero_done, 1)
            for g in range(2):
                a_body(g, g, True)
                if g == 0:
                    load_experts()
                zero_slots(g)
            for g in range(2, HG):
                a_body(g, g % 2, True)
                if g < ZERO_PARTS:
                    zero_slots(g)
            a_body(HG, 0, True)
            for i in range(HG // 2 - 2):
                for v in range(2):
                    load_rows(2 * i + v, v, i)
                    a_body(2 * i + HG + 1 + v, 1 - v, True)
            load_rows(HG - 4, 0, HG // 2 - 2)
            a_body(NG - 3, 1, True)
            load_rows(HG - 3, 1, HG // 2 - 2)
            a_body(NG - 2, 0, False)
            load_rows(HG - 2, 0, HG // 2 - 1)
            a_body(NG - 1, 1, False)
            load_rows(HG - 1, 1, HG // 2 - 1)

            def r_load(r, u):
                sp.dma_start(by_tile(xs_in[u]),
                             x_sorted[bass.ds(r * W, W), :].rearrange("(t p) d -> p t d", p=P)).then_inc(r_in[u], 16)

            def r_next(r, u):
                sp.wait_ge(r_xT_ps, r + 1)
                r_load(r + 2, u)

            for u in range(2):
                sp.wait_ge(scattered[u], 16 * G * (HG // 2))
            sp.wait_ge(s_add, NG)
            sp.wait_ge(a_rows, 16 * NG)
            r_load(0, 0)
            r_load(1, 1)
            load_rows(HG, 0, HG // 2)
            load_rows(HG + 1, 1, HG // 2)
            with sp.Fori(0, HR // 2 - 2) as i:
                for u in range(2):
                    r_next(2 * i + u, u)
                    load_rows(HG + 2 + 2 * i + u, u, HG // 2 + 1 + i)
            for u in range(2):
                r_next(HR - 4 + u, u)
            for u in range(2):
                sp.wait_ge(scattered[u], 16 * G * (NG // 2))
            with sp.Fori(HR // 2 - 1, NR // 2 - 1) as i:
                for u in range(2):
                    r_next(2 * i + u, u)

            with sp.Fori(0, NG // 2) as i:
                for u in range(2):
                    sp.wait_ge(t_res, 2 * i + u + 1)
                    sp.dma_start(out[bass.ds((2 * i + u) * G, G), :, :].rearrange("b s d -> s b d"),
                                 by_tile(res[u])).then_inc(stored[u], 16)
            for u in range(2):
                sp.wait_ge(stored[u], 16 * (NG // 2 + 1))
            sp.wait_ge(a_rows, 16 * NG)
            sp.wait_ge(zeroed, 16 * ZERO_PARTS)

        @block.gpsimd
        def _(pool):
            pool.memset(neg_half[:, :], -0.5).then_inc(half_done, 1)
            pool.memset(eps[:, :], EPS).then_inc(half_done, 1)
            pool.memset(zeros, 0.0).then_inc(zero_done, 1)
            pool.memset(all_ones[:, :], 1.0).then_inc(ones_done, 1)
            pool.wait_ge(half_done, 2)

            def rstd(s, g, mv_done, ve_done, rs_done):
                pool.wait_ge(mv_done, g + 1)
                pool.tensor_tensor(ve[:, s, :], mv[:, s, :, 1], eps[:, :], ALU.add).then_inc(ve_done, 1)
                pool.wait_ge(ve_done, g + 1)
                pool.tensor_tensor(rs[:, s, :], ve[:, s, :], neg_half[:, :], ALU.pow).then_inc(rs_done, 1)

            def scale_rows(k, v, i):
                pool.wait_ge(k_in[v], 16 * (i + 1))
                pool.tensor_copy(idx[:, v, :], cols(POS, k * G, G))
                pool.tensor_copy(sco[:, v, :], cols(SCORE, k * G, G)).then_inc(k_idx, 1)
                pool.wait_ge(k_idx, k + 1)
                pool.tensor_tensor(by_tile(xs[v]), by_tile(xs[v]),
                                   sco[:, v, :].unsqueeze(2).to_broadcast([P, G, P]), ALU.mult).then_inc(k_scaled, 1)

            def scatter(k, v, tiles):
                pool.wait_ge(k_scaled, k + 1)
                pool.sem_inc(pool_passed, 1)
                for j in tiles:
                    pool.indirect_dma_start(x_sorted, bass.IndirectOffsetOnAxis(ap=idx[:, v, j:j + 1], axis=0),
                                            tile(xs[v], j), None).then_inc(scattered[v], 16)

            def a_body(f, g, l, m, u, k):
                if k is not None:
                    v = k % 2 if isinstance(k, int) else u
                if f is not None:
                    rstd(0, f, a_mv1, a_ve1, a_rs1)
                if k is not None:
                    scale_rows(k, v, k // 2)
                    scatter(k, v, (0, 1))
                if g is not None:
                    rstd(1, g, a_mv2, a_ve2, a_rs2)
                if k is not None:
                    scatter(k, v, (2, 3))

            def a_route(h):
                pool.wait_ge(zeroed, 16 * ZERO_PARTS)
                pool.wait_ge(routed, h + 1)

            phase_a(pool, a_body, a_route)

            pool.wait_ge(routed, 2)
            with pool.Fori(0, HG // 2) as i:
                for v in range(2):
                    k = 2 * i + HG + v
                    scale_rows(k, v, HG // 2 + i)
                    scatter(k, v, range(G))

            for u in range(2):
                pool.wait_ge(r_out[u], 16 * (NR // 2 + 1))

            def gather(h, u):
                pool.tensor_copy(idx[:, u, :], cols(POS, h * G, G)).then_inc(c_idx, 1)
                pool.wait_ge(c_idx, h + 1)
                pool.sem_inc(pool_passed, 1)
                for j in range(G):
                    pool.indirect_dma_start(tile(ys[u], j), None, y_sorted,
                                            bass.IndirectOffsetOnAxis(ap=idx[:, u, j:j + 1], axis=0)
                                            ).then_inc(y_in[u], 16)

            for u in range(2):
                pool.wait_ge(scattered[u], 16 * G * (NG // 2))
            gather(0, 0)
            gather(1, 1)
            rstd(0, 0, c_mv3, c_ve3, c_rs3)
            gather(2, 0)
            rstd(1, 0, c_mv4, c_ve4, c_rs4)
            rstd(0, 1, c_mv3, c_ve3, c_rs3)

            def c_body(g, u, stores):
                if not last(g, 2):
                    rstd(0, g + 2, c_mv3, c_ve3, c_rs3)
                    if not last(g, 3):
                        gather(g + 3, 1 - u)
                if not last(g, 1):
                    rstd(1, g + 1, c_mv4, c_ve4, c_rs4)

            phase_c(pool, c_body)

        @block.scalar
        def _(act):
            for dst, src in A_WEIGHTS:
                act.dma_start(dst, src).then_inc(w_a, 16)
            act.wait_ge(w_a, 16 * len(A_WEIGHTS))

            def a_body(f, g, l, m, u, k):
                if l is not None:
                    act.wait_ge(a_x2T_ps, l + 1)
                    if not first(l):
                        act.wait_ge(a_lg_ps, l)
                    act.activation(xn2T, bank(2), ACT.Copy).then_inc(a_x2T, 1)
                if g is not None:
                    act.wait_ge(a_max, g + 1)
                    if not first(g):
                        act.wait_ge(a_pT_ps, g)
                        act.wait_ge(a_x1, g)
                    for j in range(G):
                        i = act.activation(tile(prob, j, KEYS), tile(bank(1, KW), j, KEYS), ACT.Exp,
                                           bias=nmax[:, j:j + 1], accum_out=ssum[:, j:j + 1])
                    i.then_inc(a_exp, 1)
                if f is not None:
                    act.wait_ge(a_ctxT_ps, f + 1)
                    act.activation(ctxT[u], bank(0, KW), ACT.Copy).then_inc(a_ctxT, 1)
                if l is not None:
                    act.wait_ge(s_gu_ps, l + 1)
                    if not first(l):
                        act.wait_ge(s_y_ps, l)
                    act.activation(s_act, PS[:, 4 * 512:6 * 512], ACT.Silu).then_inc(s_sil, 1)
                if f is not None:
                    act.wait_ge(a_k_ps, f + 1)
                    act.activation(cols(KT, f * KW, KW), bank(3, KW), ACT.Identity, bias=bkc[:, :]).then_inc(a_k, 1)
                    act.wait_ge(a_xnT_ps, f + 1)
                    act.activation(xnT, bank(0), ACT.Copy).then_inc(a_xnT, 1)
                    act.wait_ge(a_qT_ps, f + 1)
                    act.activation(qT, bank(0), ACT.Identity, bias=b0c[:, :]).then_inc(a_qT, 1)

            def a_route(h):
                act.wait_ge(top_done, h + 1)
                act.activation(SCORE[:, h * HB:(h + 1) * HB], top, ACT.Sigmoid).then_inc(scored, 1)

            phase_a(act, a_body, a_route)

            def r_evac_x(r, u):
                act.wait_ge(r_xT_ps, r + 1)
                act.activation(xsT[u], bank(0), ACT.Copy).then_inc(r_xT, 1)

            def r_silu(q, v):
                act.wait_ge(r_gu_ps, q + 1)
                pair = by_tile(PS[:, 512 * (1 + 2 * v):512 * (3 + 2 * v)], 512)
                act.activation(by_tile(sg[v], FI), pair[:, :, 0:FI], ACT.Silu).then_inc(r_sg, 1)

            def r_evac_y(r, u, stores):
                act.wait_ge(r_y_ps, 2 * r + 2)
                act.wait_ge(r_out[u], 16 * (stores + 1))
                act.activation(yo[u], bank(6 + u), ACT.Copy).then_inc(r_y, 1)
                act.wait_ge(r_y, r + 1)
                act.dma_start(y_sorted[bass.ds(r * W, W), :].rearrange("(t p) d -> p t d", p=P),
                              by_tile(yo[u])).then_inc(r_out[u], 16)

            def r_body(r, u, stores):
                r_silu(2 * r, 0)
                if isinstance(r, int) and r == 1:
                    a_route(1)
                if not last_unit(r):
                    r_evac_x(r + 1, 1 - u)
                r_silu(2 * r + 1, 1)
                if not first(r):
                    r_evac_y(r - 1, 1 - u, stores)

            r_evac_x(0, 0)
            r_body(0, 0, None)
            r_body(1, 1, 0)
            r_body(2, 0, 0)
            with act.Fori(1, NR // 2 - 1) as i:
                r_body(2 * i + 1, 1, i)
                r_body(2 * i + 2, 0, i)
            r_body(NR - 1, 1, NR // 2 - 1)
            r_evac_y(NR - 1, 1, NR // 2 - 1)

            def c_xnT_evac(h):
                act.wait_ge(c_xnT_ps, h + 1)
                act.activation(xn3T, bank(5), ACT.Copy).then_inc(c_xnT, 1)

            def c_qT_evac(h):
                act.wait_ge(c_qT_ps, h + 1)
                act.activation(q1T, bank(6), ACT.Identity, bias=bqc[:, :]).then_inc(c_qT, 1)

            def c_softmax(h):
                act.wait_ge(c_maxs, h + 1)
                for j in range(G):
                    i = act.activation(tile(prob1, j, KEYS), tile(bank(7, KW), j, KEYS), ACT.Exp, scale=SCALE,
                                       bias=nmax_s[:, j:j + 1], accum_out=ssum[:, j:j + 1])
                i.then_inc(c_exp, 1)

            def c_pT_evac(h):
                act.wait_ge(c_pT_ps, h + 1)
                act.activation(prob1T, bank(5, W, KEYS), ACT.Copy).then_inc(c_pT, 1)

            def c_x4_high(h):
                act.wait_ge(c_x4T_ps, h + 1)
                act.activation(x4T_h, bank(7), ACT.Copy).then_inc(c_x4h, 1)

            def t_silu_high(g, p):
                q = TREES * g + p
                if not below(q, 2):
                    act.wait_ge(t_lo, 2 * q - 2)
                for c in range(2):
                    act.wait_ge(t_mask, 2 * q + c + 1)
                    act.activation(tile(sil[p % 2], c, W), bank(2 * (p % 2) + c), ACT.Silu,
                                   bias=b_in_c[:, 2 * p + c:2 * p + c + 1]).then_inc(t_silu, 1)
                if p == DVE_TREE:
                    return
                if not below(q, 2):
                    act.wait_ge(t_out, 2 * q - 2)
                for c in range(2):
                    act.wait_ge(t_silu, 2 * q + c + 1)
                    act.activation(tile(sil_h[p % 2], c, W), tile(sil[p % 2], c, W), ACT.Copy).then_inc(t_hi, 1)

            def t_acc_evac(g):
                act.wait_ge(t_out, 2 * TREES * (g + 1))
                if not first(g):
                    act.wait_ge(t_acc, g)
                act.activation(accT, bank(4), ACT.Copy).then_inc(t_accT, 1)

            def c_body(g, u, stores):
                for p in range(TREES):
                    if p == 7 and not last(g, 1):
                        c_x4_high(g + 1)
                    t_silu_high(g, p)
                    if p == 0 and not first(g):
                        t_acc_evac(g - 1)
                    if not last(g, 1):
                        if p == 1:
                            c_softmax(g + 1)
                        if p == 3:
                            c_pT_evac(g + 1)
                    if not last(g, 2):
                        if p == 5:
                            c_xnT_evac(g + 2)
                        if p == 6:
                            c_qT_evac(g + 2)

            c_xnT_evac(0)
            c_qT_evac(0)
            c_softmax(0)
            c_pT_evac(0)
            c_x4_high(0)
            c_xnT_evac(1)
            c_qT_evac(1)
            phase_c(act, c_body)
            t_acc_evac(NG - 1)

        @block.tensor
        def _(pe):
            pe.wait_ge(w_a, 16 * len(A_WEIGHTS))
            pe.wait_ge(cast_done, 1)
            pe.wait_ge(ones_done, 1)

            def turn(dst, src, rows, n, signal):
                for j in range(G):
                    i = pe.transpose(dst[0:n, j * rows:(j + 1) * rows], tile(src, j, n), IDENT[0:rows, 0:rows])
                i.then_inc(signal, 1)

            def a_body(f, g, l, m, u, k):
                if g is not None:
                    pe.wait_ge(a_qT, g + 1)
                    if not first(g):
                        pe.wait_ge(a_x1, g)
                    for j in range(G):
                        i = pe.matmul(tile(bank(1, KW), j, KEYS), tile(qT, j), tile(ctxT[1 - u], j, KEYS),
                                      start=True, stop=True)
                    i.then_inc(a_s_ps, 1)
                if f is not None:
                    pe.wait_ge(c_in[u], 16 * (f // 2 + 1))
                    turn(bank(0, KW), ctx_rows[u], KEYS, P, a_ctxT_ps)
                if m is not None:
                    pe.wait_ge(s_act_d, m + 1)
                    if f is not None or (isinstance(m, int) and m == NG - 3):
                        pe.wait_ge(a_v, m + 3)
                    for j in range(G):
                        for c in range(FC):
                            i = pe.matmul(tile(bank(3), j), s_act[:, c * W + j * P:c * W + (j + 1) * P],
                                          SD[:, c * P:(c + 1) * P], start=(c == 0), stop=(c == FC - 1))
                    i.then_inc(s_y_ps, 1)
                if l is not None:
                    pe.wait_ge(a_xn2, l + 1)
                    turn(bank(2), xn2, P, P, a_x2T_ps)
                    pe.wait_ge(a_x2T, l + 1)
                    for n in range(2 * FC):
                        i = pe.matmul(bank(4 + n), SGU[:, n * P:(n + 1) * P], xn2T, start=True, stop=True)
                    i.then_inc(s_gu_ps, 1)
                if g is not None:
                    pe.wait_ge(a_exp, g + 1)
                    turn(bank(2, W, KEYS), prob, P, KEYS, a_pT_ps)
                if f is not None:
                    pe.wait_ge(a_ctxT, f + 1)
                    if m is not None:
                        pe.wait_ge(s_add, m + 1)
                    pe.matmul(bank(3, KW), WK[:, :], ctxT[u], start=True, stop=True).then_inc(a_k_ps, 1)
                    pe.wait_ge(a_xn, f + 1)
                    turn(bank(0), xn, P, P, a_xnT_ps)
                    pe.wait_ge(a_k, f + 1)
                    for j in range(G):
                        i = pe.matmul(tile(bank(3, W, KEYS), j), tile(ctxT[u], j, KEYS), WV[:, :],
                                      start=True, stop=True)
                    i.then_inc(a_v_ps, 1)
                if g is not None:
                    pe.wait_ge(a_pT, g + 1)
                    for j in range(G):
                        i = pe.matmul(tile(bank(1), j), tile(probT, j), tile(ctx_rows[1 - u], j),
                                      start=True, stop=True)
                    i.then_inc(a_pv_ps, 1)
                if f is not None:
                    pe.wait_ge(a_xnT, f + 1)
                    pe.matmul(bank(0), W0T[:, :], xnT, start=True, stop=True).then_inc(a_qT_ps, 1)
                if l is not None:
                    for j in range(G):
                        i = pe.matmul(tile(bank(2, G * E), j, E), tile(xn2T, j), GATE[:, :], start=True, stop=True)
                    i.then_inc(a_lg_ps, 1)

            def a_route(h):
                pe.wait_ge(r_oh, h + 1)
                pe.matmul(bank(7, HB * E), before[:, :], onehot_b, start=True, stop=True)
                pe.matmul(bank(7)[:, HB * E:], all_ones[:, :], onehot_b, start=True, stop=True).then_inc(r_cnt, 1)
                pe.wait_ge(routed, h + 1)

            phase_a(pe, a_body, a_route)

            pe.wait_ge(w_exp, 48)
            pe.wait_ge(s_add, NG)

            def r_turn(r, u):
                pe.wait_ge(r_in[u], 16 * (r // 2 + 1))
                turn(bank(0), xs_in[u], P, P, r_xT_ps)

            def experts_of(q):
                return [pe.value_load(cols(EXPERT, 2 * q + t, 1)[0:1, :], min_val=0, max_val=E - 1) for t in range(2)]

            def r_gate_up(q, v, r, u, experts):
                pe.wait_ge(r_xT, r + 1)
                if not below(q, 2):
                    pe.wait_ge(r_act, q - 1)
                for t in range(2):
                    i = pe.matmul(bank(1 + 2 * v + t), tile(xsT[u], 2 * v + t),
                                  cols(WGU, experts[t] * (2 * FI), 2 * FI), start=True, stop=True)
                i.then_inc(r_gu_ps, 1)

            def r_turn_act(q, v):
                pe.wait_ge(r_act, q + 1)
                if not first(q):
                    pe.wait_ge(r_aT, q)
                turn(bank(5), ract[v], P, P, r_aT_ps)

            def r_down(q, v, u, experts):
                pe.wait_ge(r_aT, q + 1)
                for t in range(2):
                    for c in range(FC):
                        i = pe.matmul(tile(bank(6 + u), 2 * v + t), tile(actT[v], 2 * t + c),
                                      cols(WD, experts[t] * (FC * P) + c * P, P), start=(c == 0), stop=(c == FC - 1))
                i.then_inc(r_y_ps, 1)

            def r_body(r, u, end=False):
                q = 2 * r
                if not first(r):
                    down = experts_of(q - 1)
                if not end:
                    up = experts_of(q + 2)
                    r_turn(r + 1, 1 - u)
                r_turn_act(q, 0)
                if not first(r):
                    r_down(q - 1, 1, 1 - u, down)
                if not end:
                    r_gate_up(q + 2, 0, r + 1, 1 - u, up)
                down = experts_of(q)
                if not end:
                    up = experts_of(q + 3)
                r_turn_act(q + 1, 1)
                if not below(r, 2):
                    pe.wait_ge(r_y, r - 1)
                r_down(q, 0, u, down)
                if not end:
                    r_gate_up(q + 3, 1, r + 1, 1 - u, up)

            r_turn(0, 0)
            for q in range(2):
                r_gate_up(q, q, 0, 0, experts_of(q))
            r_body(0, 0)
            a_route(1)
            r_body(1, 1)
            r_body(2, 0)
            with pe.Fori(1, NR // 2 - 1) as i:
                r_body(2 * i + 1, 1)
                r_body(2 * i + 2, 0)
            r_body(NR - 1, 1, True)
            r_down(2 * NR - 1, 1, 1, experts_of(2 * NR - 1))

            def c_turn_x(h):
                pe.wait_ge(c_xn3, h + 1)
                turn(bank(5), xn3, P, P, c_xnT_ps)

            def c_query(h):
                pe.wait_ge(c_xnT, h + 1)
                if not first(h):
                    pe.wait_ge(c_x3, h)
                pe.matmul(bank(6), WQ[:, :], xn3T, start=True, stop=True).then_inc(c_qT_ps, 1)

            def c_scores(h):
                pe.wait_ge(c_qT, h + 1)
                for j in range(G):
                    i = pe.matmul(tile(bank(7, KW), j, KEYS), tile(q1T, j), cols(KT, h * KW + j * KEYS, KEYS),
                                  start=True, stop=True)
                i.then_inc(c_s_ps, 1)

            def c_turn_prob(h):
                pe.wait_ge(c_exp, h + 1)
                if not below(h, 2):
                    pe.wait_ge(t_res, h - 1)
                turn(bank(5, W, KEYS), prob1, P, KEYS, c_pT_ps)

            def c_values(h):
                pe.wait_ge(c_pT, h + 1)
                for j in range(G):
                    i = pe.matmul(tile(bank(6), j), tile(prob1T, j), cols(V, h * W + j * P, P), start=True, stop=True)
                i.then_inc(c_pv_ps, 1)

            def c_turn_x4(h):
                pe.wait_ge(c_xn4, h + 1)
                turn(bank(7), xn4, P, P, c_x4T_ps)

            def t_logits(g, p):
                q = TREES * g + p
                pe.wait_ge(c_x4h, g + 1)
                pe.wait_ge(c_x4l, g + 1)
                for c in range(2):
                    if not below(q, 2):
                        pe.wait_ge(t_silu, 2 * q - 3 + c)
                    dst, hi, lo = bank(2 * (p % 2) + c), tile(win_h, 2 * p + c), tile(win_l, 2 * p + c)
                    pe.matmul(dst, lo, x4T_h, start=True, stop=False, skip_group_check=True)
                    pe.matmul(dst, hi, x4T_l, start=False, stop=False, skip_group_check=True)
                    i = pe.matmul(dst, hi, x4T_h, start=False, stop=True, skip_group_check=True)
                    if c == 0:
                        i.then_inc(t_in, 1)

            def t_path(g, p):
                pe.wait_ge(t_dec, TREES * g + p + 1)
                pe.matmul(bank(2 * (p % 2)), anc_in[:, :], dec[p % 2], start=False, stop=True,
                          skip_group_check=True).then_inc(t_mask, 1)
                pe.matmul(bank(2 * (p % 2) + 1), anc_lv[:, :], dec[p % 2], start=False, stop=True,
                          skip_group_check=True).then_inc(t_mask, 1)

            def t_output(g, p):
                q = TREES * g + p
                if p == 0 and not first(g):
                    pe.wait_ge(t_accT, g)
                for c in range(2):
                    pe.wait_ge(t_lo, 2 * q + c + 1)
                    hi, lo = tile(wout_h, 2 * p + c), tile(wout_l, 2 * p + c)
                    act_h, act_l = tile(sil_h[p % 2], c, W), tile(sil_l[p % 2], c, W)
                    pe.matmul(bank(4), lo, act_h, start=(p == 0 and c == 0), stop=False)
                    pe.matmul(bank(4), hi, act_l, start=False, stop=False)
                    pe.matmul(bank(4), hi, act_h, start=False,
                              stop=(p == TREES - 1 and c == 1)).then_inc(t_out, 1)

            def c_body(g, u, stores):
                for p in range(TREES):
                    if p + 1 < TREES:
                        t_logits(g, p + 1)
                    if p == 7 and not last(g, 1):
                        c_turn_x4(g + 1)
                    t_path(g, p)
                    if p == 1 and not first(g):
                        pe.wait_ge(t_accT, g)
                        turn(bank(5), accT, P, P, t_acc)
                    if not last(g, 1):
                        if p == 0:
                            c_scores(g + 1)
                        if p == 3:
                            c_turn_prob(g + 1)
                        if p == 4:
                            c_values(g + 1)
                    if not last(g, 2):
                        if p == 5:
                            c_turn_x(g + 2)
                        if p == 6:
                            c_query(g + 2)
                    if p:
                        t_output(g, p - 1)
                    elif not first(g):
                        t_output(g - 1, TREES - 1)
                    if p == TREES - 1 and not last(g, 1):
                        t_logits(g + 1, 0)

            pe.wait_ge(r_y, NR)
            c_turn_x(0)
            c_query(0)
            c_scores(0)
            c_turn_prob(0)
            c_values(0)
            c_turn_x4(0)
            c_turn_x(1)
            c_query(1)
            t_logits(0, 0)
            phase_c(pe, c_body)
            t_output(NG - 1, TREES - 1)
            pe.wait_ge(t_accT, NG)
            turn(bank(5), accT, P, P, t_acc)

        @block.vector
        def _(dve):
            dve.wait_ge(w_a, 16 * len(A_WEIGHTS))
            dve.tensor_copy(anc_in[:, :], WA[:, C_IN:C_IN + P])
            dve.tensor_copy(anc_lv[:, :], WA[:, C_LV:C_LV + P])
            dve.tensor_copy(before[:, :], WA[:, C_BEF:C_BEF + P]).then_inc(cast_done, 1)

            def stats(s, g, st_done, mv_done):
                dve.sem_inc(dve_passed, 1)
                for j in range(G):
                    i = dve.bn_stats(st[:, s, j, :], cols(X, g * W + j * P, P))
                i.then_inc(st_done, 1)
                dve.wait_ge(st_done, g + 1)
                dve.sem_inc(dve_passed, 1)
                for j in range(G):
                    i = dve.bn_aggr(mv[:, s, j, :], st[:, s, j, :])
                i.then_inc(mv_done, 1)

            def normalise(s, g, rs_done, dst, done):
                dve.wait_ge(rs_done, g + 1)
                for j in range(G):
                    i = dve.tensor_scalar(tile(dst, j), cols(X, g * W + j * P, P), mv[:, s, j, 0:1],
                                          rs[:, s, j:j + 1], ALU.subtract, ALU.mult)
                i.then_inc(done, 1)

            def split_trees():
                dve.wait_ge(w_tree, 32)
                dve.tensor_copy(win_h, win_f)
                dve.tensor_copy(wout_h, wout_f).then_inc(tree_hi, 1)
                dve.wait_ge(tree_hi, 1)
                dve.tensor_tensor(win_l, win_f, win_h.bitcast(F32), ALU.subtract)
                dve.tensor_tensor(wout_l, wout_f, wout_h.bitcast(F32), ALU.subtract).then_inc(tree_split, 1)

            def a_body(f, g, l, m, u, k):
                if g is not None:
                    dve.wait_ge(a_s_ps, g + 1)
                    dve.tensor_reduce(nmax[:, :], by_tile(bank(1, KW), KEYS), AX.X, ALU.max,
                                      negate=True).then_inc(a_max, 1)
                if f is not None:
                    dve.wait_ge(x_in[u], 16 * (f // 2 + 1))
                    stats(0, f, a_st1, a_mv1)
                if m is not None:
                    dve.wait_ge(s_y_ps, m + 1)
                    row = cols(X, m * W, W)
                    dve.tensor_tensor(row, row, bank(3), ALU.add).then_inc(s_add, 1)
                if f is not None:
                    if not first(f):
                        dve.wait_ge(a_xnT_ps, f)
                    normalise(0, f, a_rs1, xn, a_xn)
                if g is not None:
                    dve.wait_ge(a_pT_ps, g + 1)
                    dve.tensor_copy(probT, bank(2, W, KEYS)).then_inc(a_pT, 1)
                    dve.wait_ge(a_exp, g + 1)
                    dve.reciprocal(srec[:, :], ssum[:, :]).then_inc(a_rec, 1)
                if f is not None:
                    dve.wait_ge(a_v_ps, f + 1)
                    dve.tensor_tensor(by_tile(cols(V, f * W, W)), by_tile(bank(3, W, KEYS)),
                                      bvr[:, :].unsqueeze(1).to_broadcast([KEYS, G, P]), ALU.add).then_inc(a_v, 1)
                if l is not None:
                    dve.wait_ge(s_sil, l + 1)
                    dve.tensor_tensor(s_act, s_act, PS[:, 6 * 512:8 * 512], ALU.mult).then_inc(s_act_d, 1)
                if g is not None:
                    dve.wait_ge(a_rec, g + 1)
                    dve.wait_ge(a_pv_ps, g + 1)
                    for j in range(G):
                        row = cols(X, g * W + j * P, P)
                        i = dve.scalar_tensor_tensor(out=row, in0=tile(bank(1), j), scalar=srec[:, j:j + 1],
                                                     in1=row, op0=ALU.mult, op1=ALU.add)
                    i.then_inc(a_x1, 1)
                    dve.wait_ge(a_x1, g + 1)
                    stats(1, g, a_st2, a_mv2)
                if l is not None:
                    dve.wait_ge(a_lg_ps, l + 1)
                    at = (l * (G * E) if not isinstance(l, int) else (l % HG) * (G * E))
                    dve.tensor_copy(cols(LG, at - lg_base[0], G * E) if not isinstance(l, int) else cols(LG, at, G * E),
                                    bank(2, G * E)).then_inc(a_lg, 1)
                if g is not None:
                    if not first(g):
                        dve.wait_ge(a_x2T_ps, g)
                        dve.wait_ge(a_rows, 16 * g)
                    normalise(1, g, a_rs2, xn2, a_xn2)
                if first(f):
                    split_trees()

            steps = [0]
            lg_base = [0]

            def step(ins):
                steps[0] += 1
                ins.then_inc(route, 1)
                dve.wait_ge(route, steps[0])

            def te(a):
                return a.rearrange("p (t e) -> p t e", e=E)

            def et(a):
                return a.rearrange("p (e t) -> p e t", e=E)

            def over_e(a, n=HB):
                return a.unsqueeze(2).to_broadcast([P, n, E])

            rank = c_rout[:, 0:E]
            tile_no = c_rout[:, E:E + HTILES]
            keep = c_rout[:, E + HTILES:]

            def a_route(h):
                lg_base[0] = HB * E * (h + 1)
                dve.wait_ge(a_lg, HG * (h + 1))
                dve.tensor_reduce(top, te(LG[:, :]), AX.X, ALU.max).then_inc(top_done, 1)
                dve.wait_ge(top_done, h + 1)
                step(dve.tensor_tensor(te(lead), te(LG[:, :]), over_e(top), ALU.is_ge))
                step(dve.tensor_tensor(te(lead), te(lead), rank.unsqueeze(1).to_broadcast([P, HB, E]), ALU.mult))
                step(dve.tensor_reduce(best, te(lead), AX.X, ALU.max))
                step(dve.tensor_tensor(te(onehot), te(lead), over_e(best), ALU.is_equal))
                dve.tensor_copy(onehot_b, onehot).then_inc(r_oh, 1)
                dve.wait_ge(r_cnt, h + 1)
                step(dve.tensor_copy(et(counts), bank(7)[:, HB * E:].rearrange("p (t e) -> p e t", e=E)))
                step(dve.tensor_tensor_scan(upto, keep, counts, 0.0, ALU.mult, ALU.add))
                step(dve.tensor_scalar(tiles_i, et(upto)[:, :, HB - 1], float(P - 1), None, ALU.add))
                step(dve.tensor_scalar(tiles_i, tiles_i, 7, None, ALU.logical_shift_right))
                step(dve.tensor_copy(tiles_f, tiles_i))
                step(dve.tensor_tensor_scan(tile_end, keep[:, 1:1 + E], tiles_f, 0.0, ALU.mult, ALU.add))
                step(dve.tensor_tensor(first_slot, tile_end, tiles_f, ALU.subtract))
                step(dve.tensor_scalar(first_slot, first_slot, float(P), float(P * HTILES * h), ALU.mult, ALU.add))
                step(dve.tensor_tensor(slot, upto, counts, ALU.subtract))
                step(dve.tensor_tensor(et(slot), et(slot), first_slot.unsqueeze(2).to_broadcast([P, E, HB]), ALU.add))
                step(dve.tensor_tensor(te(lead), te(bank(7, HB * E)), slot.rearrange("p (e t) -> p t e", e=E), ALU.add))
                step(dve.tensor_tensor(lead, lead, onehot, ALU.mult))
                step(dve.tensor_reduce(posf, te(lead), AX.X, ALU.add))
                dve.tensor_copy(POS[:, h * HB:(h + 1) * HB], posf)
                step(dve.tensor_tensor(te(passed), over_e(tile_no, HTILES),
                                       tile_end.unsqueeze(1).to_broadcast([P, HTILES, E]), ALU.is_ge))
                step(dve.tensor_reduce(expert_f, te(passed), AX.X, ALU.add))
                dve.wait_ge(scored, h + 1)
                dve.tensor_scalar(EXPERT[:, h * HTILES:(h + 1) * HTILES], expert_f, float(E - 1), None,
                                  ALU.min).then_inc(routed, 1)

            phase_a(dve, a_body, a_route)

            def r_mul(q, v):
                dve.wait_ge(r_sg, q + 1)
                if not below(q, 2):
                    dve.wait_ge(r_aT_ps, q - 1)
                pair = by_tile(PS[:, 512 * (1 + 2 * v):512 * (3 + 2 * v)], 512)
                dve.tensor_tensor(by_tile(ract[v], FI), by_tile(sg[v], FI), pair[:, :, FI:], ALU.mult).then_inc(r_act, 1)

            def r_evac_a(q, v):
                dve.wait_ge(r_aT_ps, q + 1)
                if not below(q, 2):
                    dve.wait_ge(r_y_ps, q - 1)
                dve.tensor_copy(actT[v], bank(5)).then_inc(r_aT, 1)

            r_mul(0, 0)
            r_mul(1, 1)
            r_evac_a(0, 0)
            r_mul(2, 0)
            a_route(1)
            r_evac_a(1, 1)
            with dve.Fori(1, NR - 1) as r:
                r_mul(2 * r + 1, 1)
                r_evac_a(2 * r, 0)
                r_mul(2 * r + 2, 0)
                r_evac_a(2 * r + 1, 1)
            r_mul(2 * NR - 1, 1)
            r_evac_a(2 * NR - 2, 0)
            r_evac_a(2 * NR - 1, 1)

            def c_add_routed(h, u):
                dve.wait_ge(y_in[u], 16 * G * (h // 2 + 1))
                row = cols(X, h * W, W)
                dve.tensor_tensor(row, row, ys[u], ALU.add).then_inc(c_x2, 1)

            def c_stats3(h):
                dve.wait_ge(c_x2, h + 1)
                stats(0, h, c_st3, c_mv3)

            def c_norm3(h):
                if not first(h):
                    dve.wait_ge(c_xnT_ps, h)
                normalise(0, h, c_rs3, xn3, c_xn3)

            def c_max_scores(h):
                dve.wait_ge(c_s_ps, h + 1)
                dve.tensor_reduce(nmax[:, :], by_tile(bank(7, KW), KEYS), AX.X, ALU.max, negate=True).then_inc(c_max, 1)
                dve.wait_ge(c_max, h + 1)
                dve.tensor_scalar(nmax_s[:, :], nmax[:, :], SCALE, None, ALU.mult).then_inc(c_maxs, 1)

            def c_attended(h):
                dve.wait_ge(c_exp, h + 1)
                dve.reciprocal(srec[:, :], ssum[:, :]).then_inc(c_rec, 1)
                dve.wait_ge(c_rec, h + 1)
                dve.wait_ge(c_pv_ps, h + 1)
                for j in range(G):
                    row = cols(X, h * W + j * P, P)
                    i = dve.scalar_tensor_tensor(out=row, in0=tile(bank(6), j), scalar=srec[:, j:j + 1],
                                                 in1=row, op0=ALU.mult, op1=ALU.add)
                i.then_inc(c_x3, 1)

            def c_stats4(h):
                dve.wait_ge(c_x3, h + 1)
                stats(1, h, c_st4, c_mv4)

            def c_norm4(h):
                if not first(h):
                    dve.wait_ge(c_x4T_ps, h)
                normalise(1, h, c_rs4, xn4, c_xn4)

            def c_x4_low(h):
                dve.wait_ge(c_x4h, h + 1)
                dve.tensor_tensor(x4T_l, bank(7), x4T_h.bitcast(F32), ALU.subtract).then_inc(c_x4l, 1)

            def t_decide(g, p):
                q = TREES * g + p
                dve.wait_ge(t_in, q + 1)
                if not below(q, 2):
                    dve.wait_ge(t_mask, 2 * q - 2)
                dve.tensor_scalar(dec[p % 2], bank(2 * (p % 2)), b_in_c[:, 2 * p:2 * p + 1], 0.0,
                                  ALU.add, ALU.is_gt).then_inc(t_dec, 1)

            def t_low(g, p):
                q = TREES * g + p
                if p == DVE_TREE:
                    if not first(g):
                        dve.wait_ge(t_out, 2 * q - 2)
                    for c in range(2):
                        dve.wait_ge(t_silu, 2 * q + c + 1)
                        dve.tensor_copy(tile(sil_h[p % 2], c, W), tile(sil[p % 2], c, W)).then_inc(t_hi_dve, 1)
                for c in range(2):
                    if p == DVE_TREE:
                        dve.wait_ge(t_hi_dve, 2 * g + c + 1)
                    else:
                        dve.wait_ge(t_hi, 2 * ((TREES - 1) * g + p - (p > DVE_TREE)) + c + 1)
                    dve.tensor_tensor(tile(sil_l[p % 2], c, W), tile(sil[p % 2], c, W),
                                      tile(sil_h[p % 2], c, W).bitcast(F32), ALU.subtract).then_inc(t_lo, 1)

            def t_result(g, u, stores):
                dve.wait_ge(t_acc, g + 1)
                dve.wait_ge(stored[u], 16 * (stores + 1))
                dve.tensor_tensor(res[u], cols(X, g * W, W), bank(5), ALU.add).then_inc(t_res, 1)

            def c_body(g, u, stores):
                for p in range(TREES):
                    if p:
                        t_low(g, p - 1)
                    elif not first(g):
                        t_low(g - 1, TREES - 1)
                    if p + 1 < TREES:
                        t_decide(g, p + 1)
                    elif not last(g, 1):
                        c_x4_low(g + 1)
                        t_decide(g + 1, 0)
                    if p == 2 and not first(g):
                        t_result(g - 1, 1 - u, stores)
                    if not last(g, 1):
                        if p == 1:
                            c_max_scores(g + 1)
                        if p == 4:
                            c_attended(g + 1)
                        if p == 5:
                            c_stats4(g + 1)
                        if p == 6:
                            c_norm4(g + 1)
                    if not last(g, 2):
                        if p == 0:
                            c_add_routed(g + 2, u)
                        if p == 2:
                            c_stats3(g + 2)
                        if p == 3:
                            c_norm3(g + 2)

            c_add_routed(0, 0)
            c_stats3(0)
            c_norm3(0)
            c_max_scores(0)
            c_attended(0)
            c_stats4(0)
            c_norm4(0)
            c_x4_low(0)
            c_add_routed(1, 1)
            c_stats3(1)
            c_norm3(1)
            t_decide(0, 0)
            phase_c(dve, c_body)
            t_low(NG - 1, TREES - 1)
            t_result(NG - 1, 1, NG // 2 - 1)


_OUT = (B, P, P)


def kernel(**inputs):
    import concourse.bacc as bacc
    from concourse.bass_utils import run_bass_kernel_spmd

    a = {k: np.ascontiguousarray(v) for k, v in inputs.items()}
    nodes = 2 * P - 1

    def by_chunk(w, last):
        w = w.reshape(TREES, nodes, -1)
        pad = np.full((TREES, 1, w.shape[2]), last, w.dtype)
        return np.concatenate([w[:, :P - 1], pad, w[:, P - 1:]], 1).reshape(TREES * 2 * P, -1)

    arrays = {
        "x": a["x"], "ctx_kv": a["ctx_1024"], "w0": np.ascontiguousarray(a["L0_xattn_W"].T), "b0": a["L0_xattn_b"],
        "gate": a["L0_ffn_gate_w"], "sh_gate": a["L0_ffn_sh_gate"], "sh_up": a["L0_ffn_sh_up"],
        "sh_down": a["L0_ffn_sh_down"], "rt_gate": a["L0_ffn_rt_gate"], "rt_up": a["L0_ffn_rt_up"],
        "rt_down": a["L0_ffn_rt_down"], "wq": a["L1_xattn_Wq"], "bq": a["L1_xattn_bq"], "wk": a["L1_xattn_Wk"],
        "bk": a["L1_xattn_bk"], "wv": a["L1_xattn_Wv"], "bv": a["L1_xattn_bv"],
        "w_in": np.ascontiguousarray(by_chunk(a["L1_ffn_W_in"], 0.0).T),
        "b_in": np.ascontiguousarray(by_chunk(a["L1_ffn_b_in"], 1.0).reshape(2 * TREES, P).T),
        "w_out": by_chunk(np.ascontiguousarray(a["L1_ffn_W_out"].T), 0.0),
        "const": constants(),
    }
    nc = bacc.Bacc("TRN2", target_bir_lowering=False, num_devices=1)
    args = [nc.dram_tensor(f"in_{k}", v.shape, mybir.dt.from_np(v.dtype), kind="ExternalInput").ap()
            for k, v in arrays.items()]
    out = nc.dram_tensor("out_0", _OUT, F32, kind="ExternalOutput").ap()
    program(nc, *args, out)
    r = run_bass_kernel_spmd(nc, [{f"in_{k}": v for k, v in arrays.items()}], core_ids=[0])
    return r.results[0]["out_0"]
```

```python
from contextlib import ExitStack

import numpy as np

import concourse.bass as bass
from concourse import mybir

F32 = mybir.dt.float32
F32R = mybir.dt.float32r
BF16 = mybir.dt.bfloat16
I32 = mybir.dt.int32
ALU = mybir.AluOpType
ACT = mybir.ActivationFunctionType
AX = mybir.AxisListType

P = 128
B = 64
KEYS = 120
G = 4
NG = B // G
W = G * P
KW = G * KEYS
E = 8
FI = 256
FC = FI // P
HALVES = 2
HB = B // HALVES
HG = NG // HALVES
HTILES = HB + E
SLOT_TILES = HALVES * HTILES
NR = SLOT_TILES // G
HR = NR // HALVES
TREES = 8
DEPTH = 7
BIG = float(2.0 ** 40)
EPS = 1e-5
SCALE = float(P) ** -0.5


def constants():
    ident = np.eye(P, dtype=np.float32)
    inner = np.zeros((P, P), np.float32)
    leaves = np.zeros((P, P), np.float32)
    for node in range(2 * P - 1):
        table, col = (inner, node) if node < P - 1 else (leaves, node - (P - 1))
        child = node
        while child > 0:
            parent = (child - 1) // 2
            if child == 2 * parent + 2:
                table[parent, col] += BIG
                table[P - 1, col] -= BIG
            else:
                table[parent, col] -= BIG
            child = parent
    before = np.triu(np.ones((P, P), np.float32), 1)
    rank = np.broadcast_to(np.arange(E, 0, -1, dtype=np.float32), (P, E))
    tile = np.broadcast_to(np.arange(HTILES, dtype=np.float32), (P, HTILES))
    pack = np.broadcast_to(float(E) ** (np.arange(HTILES, dtype=np.float32) % G), (P, HTILES))
    keep = np.ones((P, E, HB), np.float32)
    keep[:, :, 0] = 0.0
    return np.ascontiguousarray(np.concatenate([ident, inner, leaves, before, rank, tile, pack,
                                                keep.reshape(P, E * HB)], 1).astype(np.float32))


C_ID, C_IN, C_LV, C_BEF = 0, P, 2 * P, 3 * P
C_RANK = 4 * P
C_TILE = C_RANK + E
C_PACK = C_TILE + HTILES
C_KEEP = C_PACK + HTILES
C_END = C_KEEP + E * HB


def program(nc, x, ctx_kv, ctx_t, w0, b0, gate, sh_gate, sh_up, sh_down, rt_gate, rt_up, rt_down,
            wq, bq, wk, bk, wv, bv, w_in, b_in, w_out, const, out):
    x_sorted = [nc.dram_tensor(f"x_sorted{h}", (HTILES * P, P), F32, kind="Internal").ap() for h in range(HALVES)]
    y_sorted = [nc.dram_tensor(f"y_sorted{h}", (HTILES * P, P), F32, kind="Internal").ap() for h in range(HALVES)]
    rows2 = nc.dram_tensor("rows2", (B, P, P), F32, kind="Internal").ap()
    with ExitStack() as ctx:
        def sb(name, shape, dt=F32):
            return ctx.enter_context(nc.sbuf_tensor(name, shape, dt))

        def sem(name):
            return ctx.enter_context(nc.semaphore(name))

        def sems(name, n):
            return [sem(f"{name}{i}") for i in range(n)]

        X = sb("X", [P, B * P])
        KT = sb("KT", [P, B * KEYS])
        V = sb("V", [KEYS, B * P])
        WA = sb("WA", [P, C_RANK])
        c_rout = sb("c_rout", [P, C_END - C_RANK])
        anc_in = sb("anc_in", [P, P], BF16)
        anc_lv = sb("anc_lv", [P, P], BF16)
        before = sb("before", [P, P], BF16)
        all_ones = sb("all_ones", [P, P], BF16)
        W0T = sb("W0T", [P, P])
        WQ = sb("WQ", [P, P])
        WK = sb("WK", [P, P])
        WV = sb("WV", [P, P])
        GATE = sb("GATE", [P, E])
        SGU = sb("SGU", [P, 2 * FI])
        SD = sb("SD", [P, FC * P])
        b_in_c = sb("b_in_c", [P, 2 * TREES])
        b0c = sb("b0c", [P, 1])
        bqc = sb("bqc", [P, 1])
        bkc = sb("bkc", [P, 1])
        bvr = sb("bvr", [KEYS, P])
        neg_half = sb("neg_half", [P, G])
        eps = sb("eps", [P, G])
        SCORE = sb("SCORE", [P, B])
        POS = sb("POS", [P, B], I32)
        EXPERTS = sb("EXPERTS", [P, NR], I32)
        LG = sb("LG", [P, HB * E])
        st = sb("st", [P, 2, G, 6])
        mv = sb("mv", [P, 2, G, 2])
        ve = sb("ve", [P, 2, G])
        rs = sb("rs", [P, 2, G])
        nmax = sb("nmax", [P, G])
        ssum = sb("ssum", [P, G])
        srec = sb("srec", [P, G])
        idx = sb("idx", [P, 2, G], I32)
        sco = sb("sco", [P, 2, G])
        PS = ctx.enter_context(nc.psum_tensor("PS", [P, 8 * 512], F32))

        TREE_W, EXPERT_W = 4 * 2 * TREES * P, E * 2 * FI + E * FC * P
        WORK = TREE_W + EXPERT_W
        ARENA = WORK + 10240
        arena_base = -(-nc.sbuf_base // 32) * 32
        ctx.enter_context(nc.sbuf_tensor("arena", [P, ARENA + 8], F32))

        class Cut:
            def __init__(self, start, end):
                self.at, self.end = start, end

            def take(self, name, n, parts=P, dt=F32):
                size = n if dt != BF16 else n // 2
                t = nc.alloc_sbuf_tensor_at(name, [parts, n], dt, offset=arena_base + 4 * self.at)
                self.at += -(-size // 8) * 8
                assert self.at <= self.end, name
                return t[:, :]

            def two(self, name, n, parts=P, dt=F32):
                return [self.take(f"{name}{i}", n, parts, dt) for i in range(2)]

        def bank(i, n=512, parts=P):
            return PS[0:parts, 512 * i:512 * i + n]

        IDENT = WA[:, C_ID:C_ID + P]
        COUNTS_IN = (bank(4), bank(7))
        NODES = 2 * TREES * P
        cut = Cut(0, TREE_W // 2)
        win_f, wout_f = cut.take("win_f", NODES), cut.take("wout_f", NODES)
        cut = Cut(0, TREE_W // 2)
        win_l, wout_l = cut.take("win_l", NODES, dt=F32R), cut.take("wout_l", NODES, dt=F32R)
        cut = Cut(TREE_W // 2, TREE_W)
        win_h, wout_h = cut.take("win_h", NODES, dt=F32R), cut.take("wout_h", NODES, dt=F32R)
        cut = Cut(TREE_W // 2, TREE_W)
        SGU_h, SGU_l = (cut.take(n, 2 * FI, dt=F32R) for n in ("SGU_h", "SGU_l"))
        xn2T_h, xn2T_l = (cut.take(n, W, dt=F32R) for n in ("xn2T_h", "xn2T_l"))
        cut = Cut(TREE_W, WORK)
        WGU = cut.take("WGU", E * 2 * FI)
        WD = cut.take("WD", E * FC * P)
        cut = Cut(WORK, ARENA)
        xs = cut.two("xs", W)
        scatter_end = cut.at
        ctx_rows = cut.two("ctx_rows", W, KEYS)
        ctxT = cut.two("ctxT", KW)
        xn = cut.take("xn", W)
        xnT = cut.take("xnT", W)
        qT = cut.take("qT", W)
        prob = cut.take("prob", KW)
        probT = cut.take("probT", W, KEYS)
        xn2 = cut.take("xn2", W)
        xn2T = cut.take("xn2T", W)
        s_act = cut.take("s_act", FC * W)
        zeros = cut.take("zeros", P)
        lead = cut.take("lead", HB * E)
        onehot = cut.take("onehot", HB * E)
        slot = cut.take("slot", HB * E)
        counts = cut.take("counts", HB * E)
        upto = cut.take("upto", HB * E)
        ahead = cut.take("ahead", HB * E)
        top = cut.take("top", HB)
        best = cut.take("best", HB)
        posf = cut.take("posf", HB)
        tiles_i = cut.take("tiles_i", E, dt=I32)
        tiles_f = cut.take("tiles_f", E)
        tile_end = cut.take("tile_end", E)
        first_slot = cut.take("first_slot", E)
        passed = cut.take("passed", HTILES * E)
        expert_f = cut.take("expert_f", HTILES)
        packed = cut.take("packed", HR)
        onehot_b = cut.take("onehot_b", HB * E, dt=BF16)
        cut = Cut(scatter_end, ARENA)
        xs_in = cut.two("xs_in", W)
        xsT = cut.two("xsT", W)
        sg = cut.two("sg", 2 * FI)
        ract = cut.two("ract", 2 * FI)
        actT = cut.two("actT", 2 * FI)
        yo = cut.two("yo", W)
        ys = cut.two("ys", W)
        xn_c = cut.take("xn_c", W)
        xn3T = cut.take("xn3T", W)
        cut = Cut(cut.at - W, ARENA)
        prob1T = cut.take("prob1T", W, KEYS)
        q1T = cut.take("q1T", W)
        prob1 = cut.take("prob1", KW)
        cut = Cut(WORK, scatter_end)
        x4T_h = cut.take("x4T_h", W, dt=F32R)
        x4T_l = cut.take("x4T_l", W, dt=F32R)
        cut = Cut(TREE_W, WORK)
        sil_h = cut.two("sil_h", 2 * W, dt=F32R)
        sil_l = cut.two("sil_l", 2 * W, dt=F32R)
        sil = cut.two("sil", 2 * W)
        cut = Cut(scatter_end, ARENA)
        accT = cut.take("accT", W)
        dec = cut.two("dec", W, dt=BF16)
        res = cut.two("res", W)

        x_in, c_in, ct_in = sems("x_in", 2), sems("c_in", 2), sems("ct_in", 2)
        w_id, w_tree, w_exp = sem("w_id"), sem("w_tree"), sem("w_exp")
        w_att, w_late = sem("w_att"), sem("w_late")
        cast_done, zero_done, zeroed, half_done, ones_done, tree_hi, tree_split = (
            sem(n) for n in ("cast_done", "zero_done", "zeroed", "half_done", "ones_done", "tree_hi", "tree_split"))
        (a_k_ps, a_k, a_v_ps, a_v, a_st1, a_mv1, a_ve1, a_rs1, a_xn, a_xnT_ps, a_xnT, a_qT_ps, a_qT,
         a_s_ps, a_max, a_exp, a_pT_ps, a_pT, a_pv_ps, a_rec, a_x1, a_st2, a_mv2, a_ve2, a_rs2, a_xn2, a_rows,
         a_x2T_ps, a_x2h, a_x2l, a_x2T, a_lg_ps,
         a_lg) = (sem(n) for n in (
             "a_k_ps", "a_k", "a_v_ps", "a_v", "a_st1", "a_mv1", "a_ve1", "a_rs1", "a_xn",
             "a_xnT_ps", "a_xnT", "a_qT_ps", "a_qT", "a_s_ps", "a_max", "a_exp", "a_pT_ps", "a_pT", "a_pv_ps", "a_rec",
             "a_x1", "a_st2", "a_mv2", "a_ve2", "a_rs2", "a_xn2", "a_rows", "a_x2T_ps", "a_x2h", "a_x2l", "a_x2T",
             "a_lg_ps", "a_lg"))
        s_gu_ps, s_sil, s_act_d, s_y_ps, s_add, s_w_hi, s_w = (
            sem(n) for n in ("s_gu_ps", "s_sil", "s_act_d", "s_y_ps", "s_add", "s_w_hi", "s_w"))
        top_done, route_step, r_oh, r_cnt, r_read, scored, placed, routed, dve_passed, pool_passed = (
            sem(n) for n in ("top_done", "route_step", "r_oh", "r_cnt", "r_read", "scored", "placed", "routed",
                             "dve_passed", "pool_passed"))
        k_idx, k_scaled, k_in, scattered = sem("k_idx"), sem("k_scaled"), sems("k_in", 2), sems("scattered", 2)
        r_in, r_out = sems("r_in", 2), sems("r_out", 2)
        r_xT_ps, r_xT, r_gu_ps, r_sg, r_act, r_aT_ps, r_aT, r_y_ps, r_y = (sem(n) for n in (
            "r_xT_ps", "r_xT", "r_gu_ps", "r_sg", "r_act", "r_aT_ps", "r_aT", "r_y_ps", "r_y"))
        y_in, stored = sems("y_in", 2), sems("stored", 2)
        (c_idx, c_x2, c_st3, c_mv3, c_ve3, c_rs3, c_xn3, c_xnT_ps, c_xnT, c_qT_ps, c_qT, c_s_ps, c_max, c_shift, c_exp,
         c_sum, c_pT_ps, c_pT, c_pv_ps, c_rec, c_x3, c_st4, c_mv4, c_ve4, c_rs4, c_xn4, c_x4T_ps, c_x4h, c_x4l) = (
             sem(n) for n in (
                 "c_idx", "c_x2", "c_st3", "c_mv3", "c_ve3", "c_rs3", "c_xn3", "c_xnT_ps", "c_xnT", "c_qT_ps", "c_qT",
                 "c_s_ps", "c_max", "c_shift", "c_exp", "c_sum", "c_pT_ps", "c_pT", "c_pv_ps", "c_rec", "c_x3", "c_st4",
                 "c_mv4", "c_ve4", "c_rs4", "c_xn4", "c_x4T_ps", "c_x4h", "c_x4l"))
        t_in, t_dec, t_mask, t_silu, t_hi, t_hi_dve, t_lo, t_out, t_acc, t_accT, t_res = (sem(n) for n in (
            "t_in", "t_dec", "t_mask", "t_silu", "t_hi", "t_hi_dve", "t_lo", "t_out", "t_acc", "t_accT", "t_res"))

        block = ctx.enter_context(nc.Block())

        def cols(a, start, n):
            return a[:, start:start + n] if isinstance(start, int) else a[:, bass.ds(start, n)]

        def tile(a, j, n=P):
            return a[:, j * n:(j + 1) * n]

        def by_tile(a, n=P):
            return a.rearrange("p (t n) -> p t n", n=n)

        def slots(tensors, r, h):
            return tensors[h][bass.ds((r - h * HR) * W, W), :].rearrange("(t p) d -> p t d", p=P)

        def first(g):
            return isinstance(g, int) and g == 0

        def below(g, n):
            return isinstance(g, int) and g < n

        def last(g, n):
            return isinstance(g, int) and g >= NG - n

        def last_unit(r):
            return isinstance(r, int) and r == NR - 1

        DVE_TREE = 1

        def phase_a(body, eng):
            body(0, None, None, None, 0)
            body(1, 0, None, None, 1)
            body(2, 1, 0, None, 0)
            with eng.Fori(0, HG // 2 - 1) as i:
                for u in range(2):
                    f = 2 * i + 3 + u
                    body(f, f - 1, f - 2, f - 3, 1 - u)
            body(HG + 1, HG, HG - 1, HG - 2, 1)
            for f, route in ((HG + 2, "choose"), (HG + 3, "count"), (HG + 4, "place")):
                body(f, f - 1, f - 2, f - 3, f % 2, (), route)
            for f in range(HG + 5, NG):
                k = 2 * (f - HG - 5)
                body(f, f - 1, f - 2, f - 3, f % 2, (k, k + 1))
            body(None, NG - 1, NG - 2, NG - 3, 0, (HG - 2, HG - 1), "pack")
            body(None, None, NG - 1, NG - 2, 1)
            body(None, None, None, NG - 1, 0, (), "all")

        FIRST_EARLY = HR + 2

        def c_bank(h, n, b):
            return 7 if below(h, n) else b

        def phase_c(eng, body):
            body(0, 0, None)
            with eng.Fori(0, NG // 2 - 2) as i:
                body(2 * i + 1, 1, i)
                body(2 * i + 2, 0, i)
            for g in range(NG - 3, NG):
                body(g, g % 2, (g - 1) // 2)

        IDENT_W = [(WA[:, C_ID:C_IN], const[:, C_ID:C_IN])]
        ATT_W = [(WK[:, :], wk), (bkc[:, :], bk.rearrange("(p a) -> p a", a=1)), (WV[:, :], wv),
                 (bvr[:, :], bv.partition_broadcast(KEYS)), (W0T[:, :], w0),
                 (b0c[:, :], b0.rearrange("(p a) -> p a", a=1))]
        LATE_W = [(SGU[:, 0:FI], sh_gate), (SGU[:, FI:], sh_up),
                  (by_tile(SD[:, :]), sh_down.rearrange("(c i) h -> i c h", c=FC)), (GATE[:, :], gate),
                  (WQ[:, :], wq), (bqc[:, :], bq.rearrange("(p a) -> p a", a=1)),
                  (WA[:, C_IN:], const[:, C_IN:C_RANK]), (c_rout[:, :], const[:, C_RANK:C_END]), (b_in_c[:, :], b_in)]

        @block.sync
        def _(sp):
            for u in range(2):
                sp.sem_inc(r_out[u], 16)
                sp.sem_inc(stored[u], 16)

            def load_group(g, u):
                sp.dma_start(by_tile(cols(X, g * W, W)),
                             x[bass.ds(g * G, G), :, :].rearrange("b s d -> s b d")).then_inc(x_in[u], 16)
                sp.dma_start(by_tile(ctxT[u], KEYS),
                             ctx_t[bass.ds(g * G, G), :, :].rearrange("b d s -> d b s")).then_inc(ct_in[u], 16)

            def load_context(g, u):
                sp.dma_start(by_tile(ctx_rows[u]),
                             ctx_kv[bass.ds(g * G, G), :, :].rearrange("b s d -> s b d")).then_inc(c_in[u], 16)

            load_group(0, 0)
            sp.wait_ge(w_att, 16 * len(ATT_W))
            load_group(1, 1)
            for g in range(2):
                load_context(g, g)

            gate_up = WGU.rearrange("p (e n) -> p e n", e=E)

            def zero_slots(h, start):
                n = HTILES // 2
                sp.dma_start(x_sorted[h][start * P:(start + n) * P, :].rearrange("(t p) d -> p t d", p=P),
                             zeros.unsqueeze(1).to_broadcast([P, n, P])).then_inc(zeroed, 16)

            def load_later(g):
                if g == 4:
                    zero_slots(0, 0)
                if g == 5:
                    zero_slots(0, HTILES // 2)
                if g == 6:
                    zero_slots(1, 0)
                if g == 7:
                    zero_slots(1, HTILES // 2)
                if g == 8:
                    sp.dma_start(win_f, w_in).then_inc(w_tree, 16)
                if g == 9:
                    sp.dma_start(by_tile(wout_f), w_out.rearrange("(c i) h -> i c h", c=2 * TREES)).then_inc(w_tree, 16)
                if g == 10:
                    sp.dma_start(gate_up[:, :, 0:FI], rt_gate.rearrange("e h i -> h e i")).then_inc(w_exp, 16)
                if g == 11:
                    sp.dma_start(gate_up[:, :, FI:], rt_up.rearrange("e h i -> h e i")).then_inc(w_exp, 16)
                if g == 12:
                    sp.dma_start(by_tile(WD), rt_down.rearrange("e (c i) h -> i (e c) h", c=FC)).then_inc(w_exp, 16)

            def load_rows(k, v, i):
                if not below(i, 1):
                    sp.wait_ge(scattered[v], 16 * G * i)
                sp.wait_ge(a_rows, 16 * (k + 1))
                sp.dma_start(by_tile(xs[v]), rows2[bass.ds(k * G, G), :, :].rearrange("b s d -> s b d")
                             ).then_inc(k_in[v], 16)

            def a_body(g, v, load):
                if load:
                    sp.wait_ge(a_s_ps, g + 1)
                    load_group(g + 2, v)
                    sp.wait_ge(a_pv_ps, g + 1)
                    load_context(g + 2, v)
                sp.wait_ge(a_xn2, g + 1)
                sp.dma_start(rows2[bass.ds(g * G, G), :, :].rearrange("b s d -> s b d"),
                             by_tile(xn2)).then_inc(a_rows, 16)

            sp.wait_ge(zero_done, 1)
            with sp.Fori(0, 2) as i:
                a_body(2 * i, 0, True)
                a_body(2 * i + 1, 1, True)
            for g in range(4, NG):
                if g == HG:
                    load_rows(0, 0, 0)
                    load_rows(1, 1, 0)
                if g > HG + 4:
                    i = g - HG - 4
                    load_rows(2 * i, 0, i)
                    load_rows(2 * i + 1, 1, i)
                load_later(g)
                a_body(g, g % 2, g < NG - 2)

            def r_load(r, u, h):
                sp.dma_start(by_tile(xs_in[u]),
                             slots(x_sorted, r, h)).then_inc(r_in[u], 16)

            def r_next(r, u, h):
                sp.wait_ge(r_xT_ps, r + 1)
                r_load(r + 2, u, h)

            for u in range(2):
                sp.wait_ge(scattered[u], 16 * G * (HG // 2))
            sp.wait_ge(a_pv_ps, NG)
            r_load(0, 0, 0)
            r_load(1, 1, 0)
            load_rows(HG, 0, HG // 2)
            load_rows(HG + 1, 1, HG // 2)
            for u in range(2):
                r_next(u, u, 0)
            with sp.Fori(0, HR // 2 - 2) as i:
                for u in range(2):
                    r_next(2 * i + 2 + u, u, 0)
                    load_rows(HG + 2 + 2 * i + u, u, HG // 2 + 1 + i)
            for u in range(2):
                sp.wait_ge(scattered[u], 16 * G * (NG // 2))
            with sp.Fori(HR // 2 - 1, NR // 2 - 1) as i:
                for u in range(2):
                    r_next(2 * i + u, u, 1)

            with sp.Fori(0, NG // 2) as i:
                for u in range(2):
                    sp.wait_ge(t_res, 2 * i + u + 1)
                    sp.dma_start(out[bass.ds((2 * i + u) * G, G), :, :].rearrange("b s d -> s b d"),
                                 by_tile(res[u])).then_inc(stored[u], 16)
            for u in range(2):
                sp.wait_ge(stored[u], 16 * (NG // 2 + 1))
            sp.wait_ge(a_rows, 16 * NG)
            sp.wait_ge(zeroed, 16 * 4)

        @block.gpsimd
        def _(pool):
            pool.memset(neg_half[:, :], -0.5).then_inc(half_done, 1)
            pool.memset(eps[:, :], EPS).then_inc(half_done, 1)
            pool.memset(zeros, 0.0).then_inc(zero_done, 1)
            pool.memset(all_ones[:, :], 1.0).then_inc(ones_done, 1)
            pool.wait_ge(half_done, 2)

            def rstd(s, g, mv_done, ve_done, rs_done):
                pool.wait_ge(mv_done, g + 1)
                pool.tensor_tensor(ve[:, s, :], mv[:, s, :, 1], eps[:, :], ALU.add).then_inc(ve_done, 1)
                pool.wait_ge(ve_done, g + 1)
                pool.tensor_tensor(rs[:, s, :], ve[:, s, :], neg_half[:, :], ALU.pow).then_inc(rs_done, 1)

            def scale_rows(k, v, i):
                pool.wait_ge(k_in[v], 16 * (i + 1))
                pool.tensor_copy(idx[:, v, :], cols(POS, k * G, G))
                pool.tensor_copy(sco[:, v, :], cols(SCORE, k * G, G)).then_inc(k_idx, 1)
                pool.wait_ge(k_idx, k + 1)
                pool.tensor_tensor(by_tile(xs[v]), by_tile(xs[v]),
                                   sco[:, v, :].unsqueeze(2).to_broadcast([P, G, P]), ALU.mult).then_inc(k_scaled, 1)

            def scatter(k, v, h):
                pool.wait_ge(k_scaled, k + 1)
                pool.sem_inc(pool_passed, 1)
                for j in range(G):
                    pool.indirect_dma_start(x_sorted[h], bass.IndirectOffsetOnAxis(ap=idx[:, v, j:j + 1], axis=0),
                                            tile(xs[v], j), None).then_inc(scattered[v], 16)

            def a_body(f, g, l, m, u, units=(), route=None):
                if f is not None:
                    rstd(0, f, a_mv1, a_ve1, a_rs1)
                if units:
                    if units[0] == 0:
                        pool.wait_ge(zeroed, 16 * 4)
                        pool.wait_ge(placed, 1)
                        pool.wait_ge(scored, 1)
                    scale_rows(units[0], 0, units[0] // 2)
                    scatter(units[0], 0, 0)
                    scale_rows(units[1], 1, units[0] // 2)
                if g is not None:
                    rstd(1, g, a_mv2, a_ve2, a_rs2)
                if units:
                    scatter(units[1], 1, 0)

            phase_a(a_body, pool)

            pool.wait_ge(placed, 2)
            pool.wait_ge(scored, 2)
            with pool.Fori(0, HG // 2) as i:
                for v in range(2):
                    k = 2 * i + HG + v
                    scale_rows(k, v, HG // 2 + i)
                    scatter(k, v, 1)

            def gather(h, u, half):
                pool.tensor_copy(idx[:, u, :], cols(POS, h * G, G)).then_inc(c_idx, 1)
                pool.wait_ge(c_idx, h + 1)
                pool.sem_inc(pool_passed, 1)
                for j in range(G):
                    pool.indirect_dma_start(tile(ys[u], j), None, y_sorted[half],
                                            bass.IndirectOffsetOnAxis(ap=idx[:, u, j:j + 1], axis=0)
                                            ).then_inc(y_in[u], 16)

            for u in range(2):
                pool.wait_ge(scattered[u], 16 * G * (NG // 2))
            for u in range(2):
                pool.wait_ge(r_out[u], 16 * (HR // 2 + 1))
            gather(0, 0, 0)
            gather(1, 1, 0)
            rstd(0, 0, c_mv3, c_ve3, c_rs3)
            gather(2, 0, 0)
            rstd(1, 0, c_mv4, c_ve4, c_rs4)
            rstd(0, 1, c_mv3, c_ve3, c_rs3)
            for u in range(2):
                pool.wait_ge(r_out[u], 16 * (NR // 2 + 1))

            def c_body(g, u, half):
                if not last(g, 2):
                    rstd(0, g + 2, c_mv3, c_ve3, c_rs3)
                    if not last(g, 3):
                        gather(g + 3, 1 - u, half)
                if not last(g, 1):
                    rstd(1, g + 1, c_mv4, c_ve4, c_rs4)

            c_body(0, 0, 0)
            for half, start, end in ((0, 0, HG // 2 - 2), (1, HG // 2 - 2, NG // 2 - 2)):
                with pool.Fori(start, end) as i:
                    c_body(2 * i + 1, 1, half)
                    c_body(2 * i + 2, 0, half)
            for g in range(NG - 3, NG):
                c_body(g, g % 2, 1)

        @block.scalar
        def _(act):
            for weights, done in ((ATT_W, w_att), (IDENT_W, w_id), (LATE_W, w_late)):
                for dst, src in weights:
                    act.dma_start(dst, src).then_inc(done, 16)

            def r_evac_x(r, u):
                act.wait_ge(r_xT_ps, r + 1)
                act.activation(xsT[u], bank(0), ACT.Copy).then_inc(r_xT, 1)

            def a_body(f, g, l, m, u, units=(), route=None):
                if l is not None:
                    act.wait_ge(a_x2T_ps, l + 1)
                    if not first(l):
                        act.wait_ge(a_lg_ps, l)
                    act.activation(xn2T_h, bank(2), ACT.Copy).then_inc(a_x2h, 1)
                if g is not None:
                    act.wait_ge(a_max, g + 1)
                    if not first(g):
                        act.wait_ge(a_pT_ps, g)
                        act.wait_ge(a_x1, g)
                    for j in range(G):
                        i = act.activation(tile(prob, j, KEYS), tile(bank(1, KW), j, KEYS), ACT.Exp,
                                           bias=nmax[:, j:j + 1], accum_out=ssum[:, j:j + 1])
                    i.then_inc(a_exp, 1)
                if l is not None:
                    act.wait_ge(a_x2l, l + 1)
                    act.activation(xn2T, bank(2), ACT.Copy).then_inc(a_x2T, 1)
                if f is not None:
                    if first(f):
                        act.wait_ge(w_att, 16 * len(ATT_W))
                    act.wait_ge(a_k_ps, f + 1)
                    act.activation(cols(KT, f * KW, KW), bank(0, KW), ACT.Identity, bias=bkc[:, :]).then_inc(a_k, 1)
                    act.wait_ge(a_xnT_ps, f + 1)
                    act.activation(xnT, bank(0), ACT.Copy).then_inc(a_xnT, 1)
                if l is not None:
                    act.wait_ge(s_gu_ps, l + 1)
                    if not first(l):
                        act.wait_ge(s_y_ps, l)
                    act.activation(s_act, PS[:, 4 * 512:6 * 512], ACT.Silu).then_inc(s_sil, 1)
                if f is not None:
                    act.wait_ge(a_qT_ps, f + 1)
                    act.activation(qT, bank(0), ACT.Identity, bias=b0c[:, :]).then_inc(a_qT, 1)
                if route == "all":
                    r_evac_x(0, 0)
                if route in ("choose", "all"):
                    h = int(route == "all")
                    act.wait_ge(top_done, h + 1)
                    act.activation(SCORE[:, h * HB:(h + 1) * HB], top, ACT.Sigmoid).then_inc(scored, 1)

            phase_a(a_body, act)

            def c_xnT_evac(h):
                act.wait_ge(c_xnT_ps, h + 1)
                if not first(h):
                    act.wait_ge(c_pv_ps, h)
                act.activation(xn3T, bank(c_bank(h, 2, 5)), ACT.Copy).then_inc(c_xnT, 1)

            def c_qT_evac(h):
                act.wait_ge(c_qT_ps, h + 1)
                act.activation(q1T, bank(c_bank(h, 2, 6)), ACT.Identity, bias=bqc[:, :]).then_inc(c_qT, 1)

            def c_softmax(h):
                act.wait_ge(c_shift, h + 1)
                act.activation(prob1, prob1, ACT.Exp, scale=SCALE).then_inc(c_exp, 1)

            def c_pT_evac(h):
                act.wait_ge(c_pT_ps, h + 1)
                act.wait_ge(c_qT_ps, h + 1)
                act.activation(prob1T, bank(c_bank(h, 1, 5), W, KEYS), ACT.Copy).then_inc(c_pT, 1)

            def c_x4_high(h):
                act.wait_ge(c_x4T_ps, h + 1)
                act.activation(x4T_h, bank(7), ACT.Copy).then_inc(c_x4h, 1)

            def r_silu(q, v):
                act.wait_ge(r_gu_ps, q + 1)
                pair = by_tile(PS[:, 512 * (1 + 2 * v):512 * (3 + 2 * v)], 512)
                act.activation(by_tile(sg[v], FI), pair[:, :, 0:FI], ACT.Silu).then_inc(r_sg, 1)

            def r_evac_y(r, u, stores, h):
                act.wait_ge(r_y_ps, 2 * r + 2)
                act.wait_ge(r_out[u], 16 * (stores + 1))
                act.activation(yo[u], bank(6), ACT.Copy).then_inc(r_y, 1)
                act.wait_ge(r_y, r + 1)
                act.dma_start(slots(y_sorted, r, h),
                              by_tile(yo[u])).then_inc(r_out[u], 16)

            def r_body(r, u, stores):
                r_silu(2 * r, 0)
                if not last_unit(r):
                    r_evac_x(r + 1, 1 - u)
                r_silu(2 * r + 1, 1)
                if not first(r):
                    r_evac_y(r - 1, 1 - u, stores, 1 if isinstance(r, int) and r > HR else 0)

            r_body(0, 0, None)
            with act.Fori(0, HR // 2) as i:
                r_body(2 * i + 1, 1, i)
                r_body(2 * i + 2, 0, i)
            for r in range(HR + 1, NR):
                r_body(r, r % 2, (r - 1) // 2)
                if r == FIRST_EARLY + 1:
                    c_xnT_evac(0)
                if r == FIRST_EARLY + 2:
                    c_qT_evac(0)
                if r == FIRST_EARLY + 3:
                    c_softmax(0)
                if r == FIRST_EARLY + 4:
                    c_pT_evac(0)
                if r == FIRST_EARLY + 6:
                    c_x4_high(0)
                if r == FIRST_EARLY + 7:
                    c_xnT_evac(1)
            r_evac_y(NR - 1, 1, NR // 2 - 1, 1)
            c_qT_evac(1)

            def t_silu_high(g, p):
                q = TREES * g + p
                if not below(q, 2):
                    act.wait_ge(t_lo, 2 * q - 2)
                for c in range(2):
                    act.wait_ge(t_mask, 2 * q + c + 1)
                    act.activation(tile(sil[p % 2], c, W), bank(2 * (p % 2) + c), ACT.Silu,
                                   bias=b_in_c[:, 2 * p + c:2 * p + c + 1]).then_inc(t_silu, 1)
                if p == DVE_TREE:
                    return
                if not below(q, 2):
                    act.wait_ge(t_out, 2 * q - 2)
                for c in range(2):
                    act.wait_ge(t_silu, 2 * q + c + 1)
                    act.activation(tile(sil_h[p % 2], c, W), tile(sil[p % 2], c, W), ACT.Copy).then_inc(t_hi, 1)

            def t_acc_evac(g):
                act.wait_ge(t_out, 2 * TREES * (g + 1))
                if not first(g):
                    act.wait_ge(t_acc, g)
                act.activation(accT, bank(4), ACT.Copy).then_inc(t_accT, 1)

            def c_body(g, u, stores):
                for p in range(TREES):
                    if p == 7 and not last(g, 1):
                        c_x4_high(g + 1)
                    t_silu_high(g, p)
                    if p == 0 and not first(g):
                        t_acc_evac(g - 1)
                    if not last(g, 1):
                        if p == 1:
                            c_softmax(g + 1)
                        if p == 3:
                            c_pT_evac(g + 1)
                    if not last(g, 2):
                        if p == 5:
                            c_xnT_evac(g + 2)
                        if p == 6:
                            c_qT_evac(g + 2)

            phase_c(act, c_body)
            t_acc_evac(NG - 1)

        @block.tensor
        def _(pe):

            def turn(dst, src, rows, n, signal):
                for j in range(G):
                    i = pe.transpose(dst[0:n, j * rows:(j + 1) * rows], tile(src, j, n), IDENT[0:rows, 0:rows])
                i.then_inc(signal, 1)

            def r_turn(r, u):
                pe.wait_ge(r_in[u], 16 * (r // 2 + 1))
                turn(bank(0), xs_in[u], P, P, r_xT_ps)

            def experts_of(r):
                word = pe.value_load(cols(EXPERTS, r, 1)[0:1, :], min_val=0, max_val=E ** G - 1)
                return [(word // E ** t) % E for t in range(G)]

            def r_gate_up(q, v, r, u, experts):
                pe.wait_ge(r_xT, r + 1)
                if not below(q, 2):
                    pe.wait_ge(r_act, q - 1)
                for t in range(2):
                    i = pe.matmul(bank(1 + 2 * v + t), tile(xsT[u], 2 * v + t),
                                  cols(WGU, experts[2 * v + t] * (2 * FI), 2 * FI), start=True, stop=True)
                i.then_inc(r_gu_ps, 1)

            def s_down(start):
                for j in (start, start + 1):
                    for c in range(FC):
                        i = pe.matmul(tile(bank(3), j), s_act[:, c * W + j * P:c * W + (j + 1) * P],
                                      SD[:, c * P:(c + 1) * P], start=(c == 0), stop=(c == FC - 1))
                return i

            def a_count(h):
                if h == 0:
                    pe.wait_ge(cast_done, 1)
                    pe.wait_ge(ones_done, 1)
                    pe.wait_ge(s_sil, HG + 1)
                pe.wait_ge(r_oh, h + 1)
                pe.matmul(COUNTS_IN[h][:, 0:HB * E], before[:, :], onehot_b, start=True, stop=True)
                pe.matmul(COUNTS_IN[h][:, HB * E:], all_ones[:, :], onehot_b, start=True, stop=True).then_inc(r_cnt, 1)

            def a_body(f, g, l, m, u, units=(), route=None):
                if route == "count":
                    a_count(0)
                if g is not None:
                    pe.wait_ge(a_qT, g + 1)
                    if not first(g):
                        pe.wait_ge(a_x1, g)
                    for j in range(G):
                        i = pe.matmul(tile(bank(1, KW), j, KEYS), tile(qT, j), tile(ctxT[1 - u], j, KEYS),
                                      start=True, stop=True)
                    i.then_inc(a_s_ps, 1)
                if f is not None:
                    if first(f):
                        pe.wait_ge(w_att, 16 * len(ATT_W))
                    pe.wait_ge(ct_in[u], 16 * (f // 2 + 1))
                    if not first(f):
                        pe.wait_ge(a_qT, f)
                    pe.matmul(bank(0, KW), WK[:, :], ctxT[u], start=True, stop=True).then_inc(a_k_ps, 1)
                if m is not None:
                    pe.wait_ge(s_act_d, m + 1)
                    if f is not None or (isinstance(m, int) and m == NG - 3):
                        pe.wait_ge(a_v, m + 3)
                    s_down(0)
                if l is not None:
                    if first(l):
                        pe.wait_ge(s_w, 1)
                    pe.wait_ge(a_xn2, l + 1)
                    turn(bank(2), xn2, P, P, a_x2T_ps)
                if m is not None:
                    s_down(2).then_inc(s_y_ps, 1)
                if route == "all":
                    pe.wait_ge(w_exp, 48)
                    pe.wait_ge(routed, 1)
                    first_experts.extend(experts_of(0))
                    pe.wait_ge(a_x1, NG)
                    pe.wait_ge(a_lg, NG)
                    r_gate_up(0, 0, 0, 0, first_experts)
                    a_count(1)
                if l is not None:
                    if route == "count":
                        pe.wait_ge(r_read, 1)
                    pe.wait_ge(a_x2h, l + 1)
                    for n in range(2 * FC):
                        w = slice(n * P, (n + 1) * P)
                        pe.matmul(bank(4 + n), SGU_l[:, w], xn2T_h, start=True, stop=False)
                        pe.matmul(bank(4 + n), SGU_h[:, w], xn2T_h, start=False, stop=False)
                    pe.wait_ge(a_x2l, l + 1)
                    for n in range(2 * FC):
                        w = slice(n * P, (n + 1) * P)
                        i = pe.matmul(bank(4 + n), SGU_h[:, w], xn2T_l, start=False, stop=True)
                    i.then_inc(s_gu_ps, 1)
                if g is not None:
                    pe.wait_ge(a_exp, g + 1)
                    if l is not None:
                        pe.wait_ge(a_x2T, l + 1)
                    turn(bank(2, W, KEYS), prob, P, KEYS, a_pT_ps)
                if f is not None:
                    if first(f):
                        pe.wait_ge(w_id, 16 * len(IDENT_W))
                    pe.wait_ge(a_xn, f + 1)
                    pe.wait_ge(a_k, f + 1)
                    turn(bank(0), xn, P, P, a_xnT_ps)
                    if m is not None:
                        pe.wait_ge(s_add, m + 1)
                    for j in range(G):
                        i = pe.matmul(tile(bank(3, W, KEYS), j), tile(ctxT[u], j, KEYS), WV[:, :],
                                      start=True, stop=True)
                    i.then_inc(a_v_ps, 1)
                if g is not None:
                    pe.wait_ge(c_in[1 - u], 16 * (g // 2 + 1))
                    pe.wait_ge(a_pT, g + 1)
                    for j in range(G):
                        i = pe.matmul(tile(bank(1), j), tile(probT, j), tile(ctx_rows[1 - u], j),
                                      start=True, stop=True)
                    i.then_inc(a_pv_ps, 1)
                if f is not None:
                    pe.wait_ge(a_xnT, f + 1)
                    pe.matmul(bank(0), W0T[:, :], xnT, start=True, stop=True).then_inc(a_qT_ps, 1)
                if l is not None:
                    pe.wait_ge(a_x2T, l + 1)
                    for j in range(G):
                        i = pe.matmul(tile(bank(2, G * E), j, E), tile(xn2T, j), GATE[:, :], start=True, stop=True)
                    i.then_inc(a_lg_ps, 1)
                if last(l, 1):
                    r_turn(0, 0)

            first_experts = []
            phase_a(a_body, pe)

            def c_turn_x(h):
                pe.wait_ge(c_xn3, h + 1)
                if below(h, 2) and h:
                    pe.wait_ge(c_x4l, h)
                turn(bank(c_bank(h, 2, 5)), xn_c, P, P, c_xnT_ps)

            def c_query(h):
                pe.wait_ge(c_xnT, h + 1)
                if not first(h):
                    pe.wait_ge(c_x3, h)
                pe.matmul(bank(c_bank(h, 2, 6)), WQ[:, :], xn3T, start=True, stop=True).then_inc(c_qT_ps, 1)

            def c_scores(h):
                pe.wait_ge(c_qT, h + 1)
                for j in range(G):
                    i = pe.matmul(tile(bank(7, KW), j, KEYS), tile(q1T, j), cols(KT, h * KW + j * KEYS, KEYS),
                                  start=True, stop=True)
                i.then_inc(c_s_ps, 1)

            def c_turn_prob(h):
                pe.wait_ge(c_exp, h + 1)
                turn(bank(c_bank(h, 1, 5), W, KEYS), prob1, P, KEYS, c_pT_ps)

            def c_values(h):
                pe.wait_ge(c_pT, h + 1)
                if not below(h, 2):
                    pe.wait_ge(t_res, h - 1)
                for j in range(G):
                    i = pe.matmul(tile(bank(c_bank(h, 1, 6)), j), tile(prob1T, j), cols(V, h * W + j * P, P),
                                  start=True, stop=True)
                i.then_inc(c_pv_ps, 1)

            def c_turn_x4(h):
                pe.wait_ge(c_xn4, h + 1)
                turn(bank(7), xn_c, P, P, c_x4T_ps)

            pe.wait_ge(s_add, NG)
            pe.wait_ge(a_rows, 16 * NG)

            def r_turn_act(q, v):
                pe.wait_ge(r_act, q + 1)
                if not first(q):
                    pe.wait_ge(r_aT, q)
                turn(bank(5), ract[v], P, P, r_aT_ps)

            def r_down(q, v, experts):
                pe.wait_ge(r_aT, q + 1)
                for t in range(2):
                    for c in range(FC):
                        i = pe.matmul(tile(bank(6), 2 * v + t), tile(actT[v], 2 * t + c),
                                      cols(WD, experts[2 * v + t] * (FC * P) + c * P, P), start=(c == 0), stop=(c == FC - 1))
                i.then_inc(r_y_ps, 1)

            def r_body(r, u, was, now=None, end=False):
                q = 2 * r
                if not end:
                    coming = experts_of(r + 1)
                    r_turn(r + 1, 1 - u)
                r_turn_act(q, 0)
                if not first(r):
                    r_down(q - 1, 1, was)
                if not end:
                    r_gate_up(q + 2, 0, r + 1, 1 - u, coming)
                if now is None:
                    now = experts_of(r)
                if isinstance(r, int):
                    if r == FIRST_EARLY + 1:
                        c_turn_x(0)
                    if r == FIRST_EARLY + 6:
                        c_turn_x4(0)
                    if r == FIRST_EARLY + 7:
                        c_turn_x(1)
                r_turn_act(q + 1, 1)
                if not first(r):
                    pe.wait_ge(r_y, r)
                r_down(q, 0, now)
                if end:
                    return now
                r_gate_up(q + 3, 1, r + 1, 1 - u, coming)
                return now, coming

            r_gate_up(1, 1, 0, 0, first_experts)
            r_body(0, 0, None, first_experts)
            with pe.Fori(0, HR // 2) as i:
                now, coming = r_body(2 * i + 1, 1, experts_of(2 * i))
                r_body(2 * i + 2, 0, now, coming)
            pe.wait_ge(routed, 2)
            now, coming = experts_of(HR), None
            for r in range(HR + 1, NR - 1):
                now, coming = r_body(r, r % 2, now, coming)
                if r == FIRST_EARLY + 1:
                    c_query(0)
                if r == FIRST_EARLY + 2:
                    c_scores(0)
                if r == FIRST_EARLY + 3:
                    c_turn_prob(0)
                if r == FIRST_EARLY + 4:
                    c_values(0)
            now = r_body(NR - 1, 1, now, coming, end=True)
            r_down(2 * NR - 1, 1, now)
            c_query(1)

            def t_logits(g, p):
                q = TREES * g + p
                pe.wait_ge(c_x4h, g + 1)
                pe.wait_ge(c_x4l, g + 1)
                for c in range(2):
                    if not below(q, 2):
                        pe.wait_ge(t_silu, 2 * q - 3 + c)
                    dst, hi, lo = bank(2 * (p % 2) + c), tile(win_h, 2 * p + c), tile(win_l, 2 * p + c)
                    pe.matmul(dst, lo, x4T_h, start=True, stop=False, skip_group_check=True)
                    pe.matmul(dst, hi, x4T_l, start=False, stop=False, skip_group_check=True)
                    i = pe.matmul(dst, hi, x4T_h, start=False, stop=True, skip_group_check=True)
                    if c == 0:
                        i.then_inc(t_in, 1)

            def t_path(g, p):
                pe.wait_ge(t_dec, TREES * g + p + 1)
                pe.matmul(bank(2 * (p % 2)), anc_in[:, :], dec[p % 2], start=False, stop=True,
                          skip_group_check=True).then_inc(t_mask, 1)
                pe.matmul(bank(2 * (p % 2) + 1), anc_lv[:, :], dec[p % 2], start=False, stop=True,
                          skip_group_check=True).then_inc(t_mask, 1)

            def t_output(g, p):
                q = TREES * g + p
                if p == 0 and not first(g):
                    pe.wait_ge(t_accT, g)
                for c in range(2):
                    pe.wait_ge(t_lo, 2 * q + c + 1)
                    hi, lo = tile(wout_h, 2 * p + c), tile(wout_l, 2 * p + c)
                    act_h, act_l = tile(sil_h[p % 2], c, W), tile(sil_l[p % 2], c, W)
                    pe.matmul(bank(4), lo, act_h, start=(p == 0 and c == 0), stop=False)
                    pe.matmul(bank(4), hi, act_l, start=False, stop=False)
                    pe.matmul(bank(4), hi, act_h, start=False,
                              stop=(p == TREES - 1 and c == 1)).then_inc(t_out, 1)

            def c_body(g, u, stores):
                for p in range(TREES):
                    if p == 3 and not first(g):
                        pe.wait_ge(t_accT, g)
                        turn(bank(6), accT, P, P, t_acc)
                    if p + 1 < TREES:
                        t_logits(g, p + 1)
                    if p == 7 and not last(g, 1):
                        c_turn_x4(g + 1)
                    t_path(g, p)
                    if not last(g, 1):
                        if p == 0:
                            c_scores(g + 1)
                        if p == 3:
                            c_turn_prob(g + 1)
                        if p == 4:
                            c_values(g + 1)
                    if not last(g, 2):
                        if p == 5:
                            c_turn_x(g + 2)
                        if p == 6:
                            c_query(g + 2)
                    if p:
                        t_output(g, p - 1)
                    elif not first(g):
                        t_output(g - 1, TREES - 1)
                    if p == TREES - 1 and not last(g, 1):
                        t_logits(g + 1, 0)

            pe.wait_ge(r_y, NR)
            pe.wait_ge(tree_split, 2)
            t_logits(0, 0)
            phase_c(pe, c_body)
            t_output(NG - 1, TREES - 1)
            pe.wait_ge(t_accT, NG)
            turn(bank(6), accT, P, P, t_acc)

        @block.vector
        def _(dve):
            def stats(s, g, st_done, mv_done):
                dve.sem_inc(dve_passed, 1)
                for j in range(G):
                    i = dve.bn_stats(st[:, s, j, :], cols(X, g * W + j * P, P))
                i.then_inc(st_done, 1)
                dve.wait_ge(st_done, g + 1)
                dve.sem_inc(dve_passed, 1)
                for j in range(G):
                    i = dve.bn_aggr(mv[:, s, j, :], st[:, s, j, :])
                i.then_inc(mv_done, 1)

            def normalise(s, g, rs_done, dst, done):
                dve.wait_ge(rs_done, g + 1)
                for j in range(G):
                    i = dve.tensor_scalar(tile(dst, j), cols(X, g * W + j * P, P), mv[:, s, j, 0:1],
                                          rs[:, s, j:j + 1], ALU.subtract, ALU.mult)
                i.then_inc(done, 1)

            def cast_constants():
                dve.wait_ge(w_late, 16 * len(LATE_W))
                dve.tensor_copy(anc_in[:, :], WA[:, C_IN:C_IN + P])
                dve.tensor_copy(anc_lv[:, :], WA[:, C_LV:C_LV + P])
                dve.tensor_copy(before[:, :], WA[:, C_BEF:C_BEF + P]).then_inc(cast_done, 1)

            def split_trees_high():
                dve.wait_ge(w_tree, 32)
                dve.tensor_copy(win_h, win_f)
                dve.tensor_copy(wout_h, wout_f).then_inc(tree_hi, 1)

            def split_trees_low(lo, f32, hi):
                dve.wait_ge(tree_hi, 1)
                dve.tensor_tensor(lo, f32, hi.bitcast(F32), ALU.subtract).then_inc(tree_split, 1)

            def split_shared():
                dve.wait_ge(w_late, 16 * len(LATE_W))
                dve.tensor_copy(SGU_h, SGU[:, :]).then_inc(s_w_hi, 1)
                dve.wait_ge(s_w_hi, 1)
                dve.tensor_tensor(SGU_l, SGU[:, :], SGU_h.bitcast(F32), ALU.subtract).then_inc(s_w, 1)

            def a_body(f, g, l, m, u, units=(), route=None):
                if route == "count":
                    a_counts(0)
                if g is not None:
                    dve.wait_ge(a_s_ps, g + 1)
                    dve.tensor_reduce(nmax[:, :], by_tile(bank(1, KW), KEYS), AX.X, ALU.max,
                                      negate=True).then_inc(a_max, 1)
                if f is not None:
                    dve.wait_ge(x_in[u], 16 * (f // 2 + 1))
                    stats(0, f, a_st1, a_mv1)
                if l is not None:
                    dve.wait_ge(a_x2h, l + 1)
                    dve.tensor_tensor(xn2T_l, bank(2), xn2T_h.bitcast(F32), ALU.subtract).then_inc(a_x2l, 1)
                if route == "all":
                    a_choose(1)
                if m is not None:
                    dve.wait_ge(s_y_ps, m + 1)
                    row = cols(X, m * W, W)
                    dve.tensor_tensor(row, row, bank(3), ALU.add).then_inc(s_add, 1)
                if route == "all":
                    a_counts(1)
                if f is not None:
                    if not first(f):
                        dve.wait_ge(a_xnT_ps, f)
                    normalise(0, f, a_rs1, xn, a_xn)
                if route == "count":
                    a_first_slots(0)
                if g is not None:
                    dve.wait_ge(a_pT_ps, g + 1)
                    dve.tensor_copy(probT, bank(2, W, KEYS)).then_inc(a_pT, 1)
                    dve.wait_ge(a_exp, g + 1)
                    dve.reciprocal(srec[:, :], ssum[:, :]).then_inc(a_rec, 1)
                if route == "choose":
                    a_choose(0)
                if route == "place":
                    a_slots(0)
                if f is not None:
                    if first(f):
                        dve.wait_ge(w_att, 16 * len(ATT_W))
                    dve.wait_ge(a_v_ps, f + 1)
                    dve.tensor_tensor(by_tile(cols(V, f * W, W)), by_tile(bank(3, W, KEYS)),
                                      bvr[:, :].unsqueeze(1).to_broadcast([KEYS, G, P]), ALU.add).then_inc(a_v, 1)
                if g is not None:
                    dve.wait_ge(a_rec, g + 1)
                    dve.wait_ge(a_pv_ps, g + 1)
                    for j in range(G):
                        row = cols(X, g * W + j * P, P)
                        i = dve.scalar_tensor_tensor(out=row, in0=tile(bank(1), j), scalar=srec[:, j:j + 1],
                                                     in1=row, op0=ALU.mult, op1=ALU.add)
                    i.then_inc(a_x1, 1)
                    dve.wait_ge(a_x1, g + 1)
                    stats(1, g, a_st2, a_mv2)
                if l is not None:
                    dve.wait_ge(s_sil, l + 1)
                    dve.tensor_tensor(s_act, s_act, PS[:, 6 * 512:8 * 512], ALU.mult).then_inc(s_act_d, 1)
                if l is not None:
                    dve.wait_ge(a_lg_ps, l + 1)
                    half = l % HG if isinstance(l, int) else l
                    dve.tensor_copy(cols(LG, half * (G * E), G * E), bank(2, G * E)).then_inc(a_lg, 1)
                if g is not None:
                    if not first(g):
                        dve.wait_ge(a_x2T_ps, g)
                        dve.wait_ge(a_rows, 16 * g)
                    normalise(1, g, a_rs2, xn2, a_xn2)
                if route == "pack":
                    a_pack(0)
                if first(f):
                    cast_constants()
                    split_shared()

            steps = [0]

            def step(ins):
                steps[0] += 1
                ins.then_inc(route_step, 1)
                dve.wait_ge(route_step, steps[0])

            def te(a):
                return a.rearrange("p (t e) -> p t e", e=E)

            def et(a):
                return a.rearrange("p (e t) -> p e t", e=E)

            def over_e(a, n=HB):
                return a.unsqueeze(2).to_broadcast([P, n, E])

            rank = c_rout[:, 0:E]
            tile_no = c_rout[:, E:E + HTILES]
            pack = c_rout[:, C_PACK - C_RANK:C_KEEP - C_RANK]
            keep = c_rout[:, C_KEEP - C_RANK:]

            def a_choose(h):
                if h == 0:
                    dve.wait_ge(w_late, 16 * len(LATE_W))
                else:
                    dve.wait_ge(scored, 1)
                dve.wait_ge(a_lg, HG * (h + 1))
                dve.tensor_reduce(top, te(LG[:, :]), AX.X, ALU.max).then_inc(top_done, 1)
                dve.wait_ge(top_done, h + 1)
                step(dve.tensor_tensor(te(lead), te(LG[:, :]), over_e(top), ALU.is_ge))
                step(dve.tensor_tensor(te(lead), te(lead), rank.unsqueeze(1).to_broadcast([P, HB, E]), ALU.mult))
                step(dve.tensor_reduce(best, te(lead), AX.X, ALU.max))
                step(dve.tensor_tensor(te(onehot), te(lead), over_e(best), ALU.is_equal))
                dve.tensor_copy(onehot_b, onehot).then_inc(r_oh, 1)

            def a_counts(h):
                dve.wait_ge(r_cnt, h + 1)
                dve.tensor_copy(et(counts), COUNTS_IN[h][:, HB * E:].rearrange("p (t e) -> p e t", e=E))
                dve.tensor_copy(ahead, COUNTS_IN[h][:, 0:HB * E]).then_inc(r_read, 1)
                dve.wait_ge(r_read, h + 1)

            def a_first_slots(h):
                step(dve.tensor_tensor_scan(upto, keep, counts, 0.0, ALU.mult, ALU.add))
                step(dve.tensor_scalar(tiles_i, et(upto)[:, :, HB - 1], float(P - 1), None, ALU.add))
                step(dve.tensor_scalar(tiles_i, tiles_i, 7, None, ALU.logical_shift_right))
                step(dve.tensor_copy(tiles_f, tiles_i))
                step(dve.tensor_tensor_scan(tile_end, keep[:, 1:1 + E], tiles_f, 0.0, ALU.mult, ALU.add))
                step(dve.tensor_tensor(first_slot, tile_end, tiles_f, ALU.subtract))
                step(dve.tensor_scalar(first_slot, first_slot, float(P), None, ALU.mult))

            def a_slots(h):
                step(dve.tensor_tensor(slot, upto, counts, ALU.subtract))
                step(dve.tensor_tensor(et(slot), et(slot), first_slot.unsqueeze(2).to_broadcast([P, E, HB]), ALU.add))
                step(dve.tensor_tensor(te(lead), te(ahead), slot.rearrange("p (e t) -> p t e", e=E), ALU.add))
                step(dve.tensor_tensor(lead, lead, onehot, ALU.mult))
                step(dve.tensor_reduce(posf, te(lead), AX.X, ALU.add))
                dve.tensor_copy(POS[:, h * HB:(h + 1) * HB], posf).then_inc(placed, 1)

            def a_pack(h):
                step(dve.tensor_tensor(te(passed), over_e(tile_no, HTILES),
                                       tile_end.unsqueeze(1).to_broadcast([P, HTILES, E]), ALU.is_ge))
                step(dve.tensor_reduce(expert_f, te(passed), AX.X, ALU.add))
                step(dve.tensor_scalar(expert_f, expert_f, float(E - 1), None, ALU.min))
                step(dve.tensor_tensor(expert_f, expert_f, pack, ALU.mult))
                step(dve.tensor_reduce(packed, by_tile(expert_f, G), AX.X, ALU.add))
                dve.tensor_copy(EXPERTS[:, h * HR:(h + 1) * HR], packed).then_inc(routed, 1)

            phase_a(a_body, dve)

            def c_add_routed(h, u):
                dve.wait_ge(y_in[u], 16 * G * (h // 2 + 1))
                row = cols(X, h * W, W)
                dve.tensor_tensor(row, row, ys[u], ALU.add).then_inc(c_x2, 1)

            def c_stats3(h):
                dve.wait_ge(c_x2, h + 1)
                stats(0, h, c_st3, c_mv3)

            def c_norm3(h):
                if not first(h):
                    dve.wait_ge(c_x4T_ps, 1 if below(h, 2) else h - 1)
                normalise(0, h, c_rs3, xn_c, c_xn3)

            def c_max_scores(h):
                dve.wait_ge(c_s_ps, h + 1)
                dve.tensor_reduce(nmax[:, :], by_tile(bank(7, KW), KEYS), AX.X, ALU.max, negate=True).then_inc(c_max, 1)
                dve.wait_ge(c_max, h + 1)
                if not first(h):
                    dve.wait_ge(c_pT_ps, h)
                dve.tensor_tensor(by_tile(prob1, KEYS), by_tile(bank(7, KW), KEYS),
                                  nmax[:, :].unsqueeze(2).to_broadcast([P, G, KEYS]), ALU.add).then_inc(c_shift, 1)

            def c_attended(h):
                dve.wait_ge(c_exp, h + 1)
                dve.tensor_reduce(ssum[:, :], by_tile(prob1, KEYS), AX.X, ALU.add).then_inc(c_sum, 1)
                dve.wait_ge(c_sum, h + 1)
                dve.reciprocal(srec[:, :], ssum[:, :]).then_inc(c_rec, 1)
                dve.wait_ge(c_rec, h + 1)
                dve.wait_ge(c_pv_ps, h + 1)
                for j in range(G):
                    row = cols(X, h * W + j * P, P)
                    i = dve.scalar_tensor_tensor(out=row, in0=tile(bank(c_bank(h, 1, 6)), j), scalar=srec[:, j:j + 1],
                                                 in1=row, op0=ALU.mult, op1=ALU.add)
                i.then_inc(c_x3, 1)

            def c_stats4(h):
                dve.wait_ge(c_x3, h + 1)
                stats(1, h, c_st4, c_mv4)

            def c_norm4(h):
                dve.wait_ge(c_xnT_ps, 1 if first(h) else NG if last(h, 1) else h + 2)
                normalise(1, h, c_rs4, xn_c, c_xn4)

            def c_x4_low(h):
                dve.wait_ge(c_x4h, h + 1)
                dve.tensor_tensor(x4T_l, bank(7), x4T_h.bitcast(F32), ALU.subtract).then_inc(c_x4l, 1)

            def r_mul(q, v):
                dve.wait_ge(r_sg, q + 1)
                if not below(q, 2):
                    dve.wait_ge(r_aT_ps, q - 1)
                pair = by_tile(PS[:, 512 * (1 + 2 * v):512 * (3 + 2 * v)], 512)
                dve.tensor_tensor(by_tile(ract[v], FI), by_tile(sg[v], FI), pair[:, :, FI:], ALU.mult).then_inc(r_act, 1)

            def r_evac_a(q, v):
                dve.wait_ge(r_aT_ps, q + 1)
                if not below(q, 2):
                    dve.wait_ge(r_y_ps, q - 1)
                dve.tensor_copy(actT[v], bank(5)).then_inc(r_aT, 1)

            def c_rows3(h):
                c_add_routed(h, h)
                c_stats3(h)

            def c_rows4(h):
                c_attended(h)
                c_stats4(h)

            def r_half(q, v):
                r_mul(q + 1, 1 - v)
                r_evac_a(q, v)

            a_first_slots(1)
            r_mul(0, 0)
            r_half(0, 0)
            a_slots(1)
            r_half(1, 1)
            a_pack(1)
            with dve.Fori(1, HR + 1) as r:
                r_half(2 * r, 0)
                r_half(2 * r + 1, 1)
            for r in range(HR + 1, NR - 1):
                r_half(2 * r, 0)
                if r == FIRST_EARLY:
                    c_rows3(0)
                if r == FIRST_EARLY + 3:
                    c_max_scores(0)
                if r == FIRST_EARLY + 5:
                    c_rows4(0)
                if r == FIRST_EARLY + 6:
                    c_rows3(1)
                r_half(2 * r + 1, 1)
                if r == HR + 1:
                    split_trees_high()
                if r == FIRST_EARLY:
                    c_norm3(0)
                if r == FIRST_EARLY + 1:
                    split_trees_low(win_l, win_f, win_h)
                if r == FIRST_EARLY + 4:
                    split_trees_low(wout_l, wout_f, wout_h)
                if r == FIRST_EARLY + 5:
                    c_norm4(0)
                if r == FIRST_EARLY + 6:
                    c_x4_low(0)
                    c_norm3(1)
            r_half(2 * NR - 2, 0)
            r_evac_a(2 * NR - 1, 1)

            def t_decide(g, p):
                q = TREES * g + p
                dve.wait_ge(t_in, q + 1)
                if not below(q, 2):
                    dve.wait_ge(t_mask, 2 * q - 2)
                dve.tensor_scalar(dec[p % 2], bank(2 * (p % 2)), b_in_c[:, 2 * p:2 * p + 1], 0.0,
                                  ALU.add, ALU.is_gt).then_inc(t_dec, 1)

            def t_low(g, p):
                q = TREES * g + p
                if p == DVE_TREE:
                    if not first(g):
                        dve.wait_ge(t_out, 2 * q - 2)
                    for c in range(2):
                        dve.wait_ge(t_silu, 2 * q + c + 1)
                        dve.tensor_copy(tile(sil_h[p % 2], c, W), tile(sil[p % 2], c, W)).then_inc(t_hi_dve, 1)
                for c in range(2):
                    if p == DVE_TREE:
                        dve.wait_ge(t_hi_dve, 2 * g + c + 1)
                    else:
                        dve.wait_ge(t_hi, 2 * ((TREES - 1) * g + p - (p > DVE_TREE)) + c + 1)
                    dve.tensor_tensor(tile(sil_l[p % 2], c, W), tile(sil[p % 2], c, W),
                                      tile(sil_h[p % 2], c, W).bitcast(F32), ALU.subtract).then_inc(t_lo, 1)

            def t_result(g, u, stores):
                dve.wait_ge(t_acc, g + 1)
                dve.wait_ge(stored[u], 16 * (stores + 1))
                dve.tensor_tensor(res[u], cols(X, g * W, W), bank(6), ALU.add).then_inc(t_res, 1)

            def c_body(g, u, stores):
                for p in range(TREES):
                    if p:
                        t_low(g, p - 1)
                    elif not first(g):
                        t_low(g - 1, TREES - 1)
                    if p + 1 < TREES:
                        t_decide(g, p + 1)
                    elif not last(g, 1):
                        c_x4_low(g + 1)
                        t_decide(g + 1, 0)
                    if p == 3 and not first(g):
                        t_result(g - 1, 1 - u, stores)
                    if not last(g, 1):
                        if p == 1:
                            c_max_scores(g + 1)
                        if p == 4:
                            c_attended(g + 1)
                        if p == 5:
                            c_stats4(g + 1)
                        if p == 6:
                            c_norm4(g + 1)
                    if not last(g, 2):
                        if p == 0:
                            c_add_routed(g + 2, u)
                        if p == 2:
                            c_stats3(g + 2)
                        if p == 3:
                            c_norm3(g + 2)

            t_decide(0, 0)
            phase_c(dve, c_body)
            t_low(NG - 1, TREES - 1)
            t_result(NG - 1, 1, NG // 2 - 1)


_OUT = (B, P, P)


def kernel(**inputs):
    import concourse.bacc as bacc
    from concourse.bass_utils import run_bass_kernel_spmd

    a = {k: np.ascontiguousarray(v) for k, v in inputs.items()}
    nodes = 2 * P - 1

    def by_chunk(w, last):
        w = w.reshape(TREES, nodes, -1)
        pad = np.full((TREES, 1, w.shape[2]), last, w.dtype)
        return np.concatenate([w[:, :P - 1], pad, w[:, P - 1:]], 1).reshape(TREES * 2 * P, -1)

    arrays = {
        "x": a["x"], "ctx_kv": a["ctx_1024"],
        "ctx_t": np.ascontiguousarray(a["ctx_1024"].transpose(0, 2, 1)),
        "w0": np.ascontiguousarray(a["L0_xattn_W"].T), "b0": a["L0_xattn_b"],
        "gate": a["L0_ffn_gate_w"], "sh_gate": a["L0_ffn_sh_gate"], "sh_up": a["L0_ffn_sh_up"],
        "sh_down": a["L0_ffn_sh_down"], "rt_gate": a["L0_ffn_rt_gate"], "rt_up": a["L0_ffn_rt_up"],
        "rt_down": a["L0_ffn_rt_down"], "wq": a["L1_xattn_Wq"], "bq": a["L1_xattn_bq"], "wk": a["L1_xattn_Wk"],
        "bk": a["L1_xattn_bk"], "wv": a["L1_xattn_Wv"], "bv": a["L1_xattn_bv"],
        "w_in": np.ascontiguousarray(by_chunk(a["L1_ffn_W_in"], 0.0).T),
        "b_in": np.ascontiguousarray(by_chunk(a["L1_ffn_b_in"], 1.0).reshape(2 * TREES, P).T),
        "w_out": by_chunk(np.ascontiguousarray(a["L1_ffn_W_out"].T), 0.0),
        "const": constants(),
    }
    nc = bacc.Bacc("TRN2", target_bir_lowering=False, num_devices=1)
    args = [nc.dram_tensor(f"in_{k}", v.shape, mybir.dt.from_np(v.dtype), kind="ExternalInput").ap()
            for k, v in arrays.items()]
    out = nc.dram_tensor("out_0", _OUT, F32, kind="ExternalOutput").ap()
    program(nc, *args, out)
    r = run_bass_kernel_spmd(nc, [{f"in_{k}": v for k, v in arrays.items()}], core_ids=[0])
    return r.results[0]["out_0"]
```
